# Optimizing a Trainium2 kernel written in Bass

```python
import numpy as np
import jax
import jax.numpy as jnp

def _softmax(x, axis=-1):
    return jax.nn.softmax(x, axis=axis)

def _gelu(x):
    return jax.nn.gelu(x, approximate=True)

def _silu(x):
    return jax.nn.silu(x)

def _sigmoid(x):
    return jax.nn.sigmoid(x)

def _layernorm(x, axis=-1, eps=1e-05):
    m = jnp.mean(x, axis=axis, keepdims=True)
    v = jnp.var(x, axis=axis, keepdims=True)
    return (x - m) / jnp.sqrt(v + eps)

def _scatter_add(tgt, idx, src, axis=0):
    return tgt.at[idx].add(src)

def _segment_sum(src, seg, n):
    return jax.ops.segment_sum(src, seg, n)
kernel_name = 'mk_xattn_ffn_d1_seqx_r8_8b2222'

def setup_inputs(seed: int=0):
    np.random.seed(seed)
    _w = jnp.asarray

    def _rec_inputs():
        import jax
        import jax.numpy as jnp
        _rk = jax.random.key(seed)
        x = -0.0003929 + 0.9999 * jax.random.normal(jax.random.fold_in(_rk, 1), (8, 128, 128), jnp.float32)
        _lenS = 128 - jax.random.randint(jax.random.fold_in(_rk, 7), (8,), 0, max(1, 128 // 4) + 1, jnp.int32)
        _lenS2 = 120 - jax.random.randint(jax.random.fold_in(_rk, 8), (8,), 0, max(1, 120 // 4) + 1, jnp.int32)
        _ctx_1024P = jax.random.normal(jax.random.fold_in(_rk, 11), (8, 16, 128), jnp.float32)
        _ctx_1024c = jax.random.dirichlet(jax.random.fold_in(_rk, 511), 0.3 * jnp.ones((16,), jnp.float32), (8, 120))
        _ctx_1024t = jnp.einsum('bsk,bkd->bsd', _ctx_1024c, _ctx_1024P)
        _ctx_1024t = _ctx_1024t * jax.lax.rsqrt(jnp.mean(jnp.square(_ctx_1024t)) + 1e-12) * 0.953939
        ctx_1024 = 2.81802e-05 + 1.00001 * (_ctx_1024t + 0.3 * jax.random.normal(jax.random.fold_in(_rk, 611), (8, 120, 128), jnp.float32))
        return (x, ctx_1024)
    x, ctx_1024 = _rec_inputs()

    def _L0_xattn_setup():
        import jax, jax.numpy as jnp
        import numpy as np
        key = jax.random.key(seed)
        ks = jax.random.split(key, 9)
        B, S, D = (8, 256, 128)
        Qd = Kd = Vd = 128
        s = 1.0 / np.sqrt(D)
        return {'query': jax.random.normal(ks[0], (B, S, D), jnp.float32), 'key': jax.random.normal(ks[1], (B, S, D), jnp.float32), 'value': jax.random.normal(ks[2], (B, S, D), jnp.float32), 'Wq': jax.random.normal(ks[3], (D, Qd), jnp.float32) * s, 'bq': jnp.zeros((Qd,), jnp.float32), 'Wk': jax.random.normal(ks[4], (D, Kd), jnp.float32) * s, 'bk': jnp.zeros((Kd,), jnp.float32), 'Wv': jax.random.normal(ks[5], (D, Vd), jnp.float32) * s, 'bv': jnp.zeros((Vd,), jnp.float32)}
    _L0_xattn_all = _L0_xattn_setup()
    _L0_xattn_in = {k: v for k, v in _L0_xattn_all.items() if k in ('Wq', 'bq', 'Wk', 'bk', 'Wv', 'bv')}
    del _L0_xattn_all

    def _L0_ffn_setup():
        import jax, jax.numpy as jnp
        import numpy as np
        NUM_EXPERTS = 8
        TOP_K = 2
        DIM = 128
        HIDDEN = 512
        B, S = (2, 128)
        key = jax.random.key(seed)
        k_x, k_g, k_1, k_2, k_3 = jax.random.split(key, 5)
        s_d = 1.0 / np.sqrt(DIM)
        s_h = 1.0 / np.sqrt(HIDDEN)
        return {'x': jax.random.normal(k_x, (B, S, DIM), dtype=jnp.float32), 'gate_w': jax.random.normal(k_g, (NUM_EXPERTS, DIM), dtype=jnp.float32) * s_d, 'w1': jax.random.normal(k_1, (NUM_EXPERTS, HIDDEN, DIM), dtype=jnp.float32) * s_d, 'w2': jax.random.normal(k_2, (NUM_EXPERTS, DIM, HIDDEN), dtype=jnp.float32) * s_h, 'w3': jax.random.normal(k_3, (NUM_EXPERTS, HIDDEN, DIM), dtype=jnp.float32) * s_d}
    _L0_ffn_all = _L0_ffn_setup()
    _L0_ffn_in = {k: v for k, v in _L0_ffn_all.items() if k in ('gate_w', 'w1', 'w2', 'w3')}
    del _L0_ffn_all
    return {'x': x, 'ctx_1024': ctx_1024, 'L0_xattn_Wq': _L0_xattn_in['Wq'], 'L0_xattn_bq': _L0_xattn_in['bq'], 'L0_xattn_Wk': _L0_xattn_in['Wk'], 'L0_xattn_bk': _L0_xattn_in['bk'], 'L0_xattn_Wv': _L0_xattn_in['Wv'], 'L0_xattn_bv': _L0_xattn_in['bv'], 'L0_ffn_gate_w': _L0_ffn_in['gate_w'], 'L0_ffn_w1': _L0_ffn_in['w1'], 'L0_ffn_w2': _L0_ffn_in['w2'], 'L0_ffn_w3': _L0_ffn_in['w3']}

def reference(x, ctx_1024, L0_xattn_Wq, L0_xattn_bq, L0_xattn_Wk, L0_xattn_bk, L0_xattn_Wv, L0_xattn_bv, L0_ffn_gate_w, L0_ffn_w1, L0_ffn_w2, L0_ffn_w3):
    import jax
    import jax.numpy as jnp

    def _L0_xattn_ref(query, key, value, Wq, bq, Wk, bk, Wv, bv):
        import jax, jax.numpy as jnp
        import numpy as np
        Q = jnp.einsum('bsd,de->bse', query, Wq) + bq
        K = jnp.einsum('bsd,de->bse', key, Wk) + bk
        V = jnp.einsum('bsd,de->bse', value, Wv) + bv
        scale = 1.0 / jnp.sqrt(jnp.asarray(K.shape[-1], Q.dtype))
        scores = jnp.einsum('bqe,bke->bqk', Q, K) * scale
        attn = jax.nn.softmax(scores, axis=-1)
        return jnp.einsum('bqk,bkv->bqv', attn, V)

    def _L0_ffn_ref(x, gate_w, w1, w2, w3):
        import jax, jax.numpy as jnp
        import numpy as np
        NUM_EXPERTS = 8
        TOP_K = 2
        DIM = 128
        HIDDEN = 512
        B, S = (2, 128)
        orig_shape = x.shape
        xt = x.reshape(-1, orig_shape[-1])
        scores = xt @ gate_w.T
        top_vals, top_idx = jax.lax.top_k(scores, TOP_K)
        top_w = jax.nn.softmax(top_vals, axis=-1)
        combine = jnp.einsum('tke,tk->te', jax.nn.one_hot(top_idx, NUM_EXPERTS, dtype=xt.dtype), top_w)
        h = jax.nn.silu(jnp.einsum('td,ehd->eth', xt, w1)) * jnp.einsum('td,ehd->eth', xt, w3)
        ye = jnp.einsum('eth,edh->etd', h, w2)
        y = jnp.einsum('te,etd->td', combine, ye)
        return y.reshape(orig_shape)
    x = x + _L0_xattn_ref(_layernorm(x, axis=-1), ctx_1024, ctx_1024, L0_xattn_Wq, L0_xattn_bq, L0_xattn_Wk, L0_xattn_bk, L0_xattn_Wv, L0_xattn_bv)
    x = x + _L0_ffn_ref(_layernorm(x, axis=-1), L0_ffn_gate_w, L0_ffn_w1, L0_ffn_w2, L0_ffn_w3)
    return x

_drawn_inputs = setup_inputs


def setup_inputs(seed=0):
    import zlib

    import numpy as np

    out = dict(_drawn_inputs(seed))
    spreads = {'L0_xattn_bq': (0.0, 0.1), 'L0_xattn_bk': (0.0, 0.1), 'L0_xattn_bv': (0.0, 0.1)}
    factors = {}
    for name, (base, spread) in spreads.items():
        noise = np.random.default_rng([zlib.crc32(name.encode()), seed]).standard_normal(out[name].shape)
        drawn = base * np.exp(spread * noise) if base else spread * noise
        out[name] = jnp.asarray(drawn.astype(out[name].dtype))
    for name, factor in factors.items():
        out[name] = (out[name] * factor).astype(out[name].dtype)
    return out
```

```python
from contextlib import ExitStack

import concourse.bass as bass
from concourse import mybir

F32 = mybir.dt.float32
BF16 = mybir.dt.bfloat16
I32 = mybir.dt.int32
U32 = mybir.dt.uint32
ALU = mybir.AluOpType
ACT = mybir.ActivationFunctionType
AX = mybir.AxisListType

P = 128


def build(nc, x, ctxT, wq, bq, wk, bk, wv, bv, gwT, w1T, w3T, w2T, out):
    B, S, D = x.shape
    C = ctxT.shape[1] // B
    E = gwT.shape[1]
    H = w1T.shape[1] // E
    HC = H // P
    assert S == P and D == P and E == 8 and 4 * P <= 512 and H == 512
    G, TG = 2, B // 2
    TOK = B * S
    K2 = 2
    NPAIR = K2 * B
    NT = K2 * TOK // P + E + 2
    EPS = 1e-5
    SCALE = float(D) ** -0.5

    x2n_rows = nc.dram_tensor("x2n_rows", [TOK, D], F32, kind="Internal").ap()

    with ExitStack() as ctx:
        def sb(name, shape, dt=F32):
            return ctx.enter_context(nc.sbuf_tensor(name, shape, dt))

        def sem(name):
            return ctx.enter_context(nc.semaphore(name))

        bank = [ctx.enter_context(nc.psum_tensor(f"bank{i}", [P, 512], F32)) for i in range(8)]

        x_sb = sb("x_sb", [P, B, D])
        ctxT_sb = sb("ctxT_sb", [P, B, C])
        wq_sb = sb("wq_sb", [P, D])
        wk_sb = sb("wk_sb", [P, D])
        wv_sb = sb("wv_sb", [P, D])
        bq_sb = sb("bq_sb", [P, 1])
        bk_sb = sb("bk_sb", [P, 1])
        bv_sb = sb("bv_sb", [P, D])
        gwT_sb = sb("gwT_sb", [P, E])
        w1_sb = sb("w1_sb", [P, E * H])
        w3_sb = sb("w3_sb", [P, E * H])
        w2_sb = sb("w2_sb", [P, E * H])
        ident = sb("ident", [P, P])
        before = sb("before", [P, P], BF16)
        ones = sb("ones", [P, P], BF16)
        iota_lane = sb("iota_lane", [P, P], I32)
        iota_tile = sb("iota_tile", [P, NT], I32)
        iota_step = sb("iota_step", [P, E], I32)
        token_id = sb("token_id", [P, B], I32)
        spare_row = sb("spare_row", [P, 1], I32)
        eps_sb = sb("eps_sb", [P, 1])
        stats = sb("stats", [P, 2, B, 6])
        meanvar = sb("meanvar", [P, 2, B, 2])
        lnvar = sb("lnvar", [P, 2, B])
        rs0 = sb("rs0", [P, 2, B])
        nw1 = sb("nw1", [P, 2, B])
        nw2 = sb("nw2", [P, 2, B])
        nw3 = sb("nw3", [P, 2, B])
        rstd = sb("rstd", [P, 2, B])
        xn = sb("xn", [P, B, D])
        xnT = sb("xnT", [P, B, P])
        qT = sb("qT", [P, B, P])
        kT = sb("kT", [P, B, C])
        v_sb = sb("v_sb", [C, B, D])
        smax = sb("smax", [P, B])
        nmax = sb("nmax", [P, B])
        probs = sb("probs", [P, B, C])
        psums = sb("psums", [P, B])
        rsum = sb("rsum", [P, B])
        pT = sb("pT", [C, B, P])
        x1 = sb("x1", [P, B, D])
        x2n = sb("x2n", [P, B, D])
        x2nT = sb("x2nT", [P, B, P])
        gate = sb("gate", [P, B, E])
        top = sb("top", [P, B, 8])
        topi = sb("topi", [P, B, 8], U32)
        vdiff = sb("vdiff", [P, B])
        vexp = sb("vexp", [P, B])
        vden = sb("vden", [P, B])
        pair_w = sb("pair_w", [P, K2, B])
        oh = sb("oh", [P, K2, B, E])
        member = sb("member", [P, B + 1, E], BF16)
        over = sb("over", [P, E, E])
        ntile = sb("ntile", [P, E])
        zeros8 = sb("zeros8", [P, E])
        tend = sb("tend", [P, E])
        base = sb("base", [P, E])
        rank = sb("rank", [P, B, E])
        pick = sb("pick", [P, K2, B, E])
        slotf = sb("slotf", [P, NPAIR])
        slot = sb("slot", [P, NPAIR], I32)
        stile = sb("stile", [P, NPAIR], I32)
        slane = sb("slane", [P, NPAIR])
        lane_oh = sb("lane_oh", [P, NPAIR, P])
        tile_oh = sb("tile_oh", [P, NPAIR, 3, NT])
        passed = sb("passed", [P, NT, E])
        expf = sb("expf", [P, NT])
        tile_expert = sb("tile_expert", [P, NT], I32)
        tcount = sb("tcount", [P, 1], I32)
        npairs_less2 = sb("npairs_less2", [P, 1], I32)
        filled = sb("filled", [P, 3, NT])
        empty = sb("empty", [P, NT])
        spare = sb("spare", [P, NT])
        gather_id = sb("gather_id", [P, NT], U32)
        add_id = sb("add_id", [P, NT], U32)
        gid = [sb(f"gid{p}", [P, 1], U32) for p in range(2)]
        aid = [sb(f"aid{p}", [P, 1], U32) for p in range(2)]
        xg = [sb(f"xg{p}", [P, D]) for p in range(2)]
        xgT = [sb(f"xgT{p}", [P, P]) for p in range(2)]
        sil = [sb(f"sil{p}", [P, H]) for p in range(2)]
        hid = [sb(f"hid{p}", [P, H]) for p in range(2)]
        hidT = [sb(f"hidT{p}", [P, H]) for p in range(2)]
        y_sb = [sb(f"y_sb{p}", [P, D]) for p in range(2)]

        ps_turn, ps_q, ps_k, ps_v, ps_s, ps_pT, ps_av, ps_rank = bank
        ps_gate = [ps_q, ps_k]
        ps_fill = ps_v
        ps_xT, ps_y, ps_hT = bank[0], bank[3], bank[6]
        ps_a, ps_b = [bank[1], bank[2]], [bank[4], bank[5]]

        s_x = [sem(f"s_x_in{g}") for g in range(G)]
        s_wqkv = sem("s_wqkv")
        s_ctx = sem("s_ctx")
        s_gw = sem("s_gw")
        s_w1, s_w3, s_w2 = sem("s_w1"), sem("s_w3"), sem("s_w2")
        s_raw = sem("s_raw")
        s_const = sem("s_const")
        s_zero = sem("s_zero")
        s_stat, s_mv, s_lnv, s_rs0 = sem("s_stat"), sem("s_mv"), sem("s_lnv"), sem("s_rs0")
        s_newton, s_xn = sem("s_newton"), sem("s_xn")
        s_turn, s_xnT = sem("s_turn"), sem("s_xnT")
        s_q, s_qT, s_k, s_kT, s_v, s_vsb = (sem(n) for n in ("s_q", "s_qT", "s_k", "s_kT", "s_v", "s_vsb"))
        s_score, s_smax, s_nmax, s_probs, s_rsum = (
            sem(n) for n in ("s_score", "s_smax", "s_nmax", "s_probs", "s_rsum"))
        s_pTp, s_pT, s_av, s_x1, s_x2n = (sem(n) for n in ("s_pTp", "s_pT", "s_av", "s_x1", "s_x2n"))
        s_turn2, s_x2nT, s_gate = sem("s_turn2"), sem("s_x2nT"), sem("s_gate")
        s_stored, s_rows = sem("s_stored"), sem("s_rows")
        s_gsb, s_top, s_topi, s_vd, s_ve, s_pw = (
            sem(n) for n in ("s_gsb", "s_top", "s_topi", "s_vd", "s_ve", "s_pw"))
        s_oh, s_mem, s_rank, s_route = sem("s_oh"), sem("s_mem"), sem("s_rank"), sem("s_route")
        s_lane, s_tile, s_fill, s_tab, s_ids = (
            sem(n) for n in ("s_lane", "s_tile", "s_fill", "s_tab", "s_ids"))
        s_ready = sem("s_ready")
        s_gid, s_aid, s_gat = sem("s_gid"), sem("s_aid"), [sem(f"s_gat{p}") for p in range(2)]
        s_xT, s_xgT, s_a, s_b, s_sil, s_hid, s_hT, s_hidT, s_y, s_ysb, s_add = (
            sem(n) for n in ("s_xT", "s_xgT", "s_a", "s_b", "s_sil", "s_hid", "s_hT", "s_hidT",
                             "s_y", "s_ysb", "s_add"))

        def grp(t, g):
            return t[:, g * TG:(g + 1) * TG]

        def pairs_of(eng):
            eng.wait_ge(s_tab, 1)
            return eng.value_load(npairs_less2[0:1, 0:1], min_val=TOK * K2 // P // 2 - 2,
                                  max_val=(NT - 2) // 2 - 2) + 2

        block = ctx.enter_context(nc.Block())

        @block.sync
        def _(sp):
            xv = x.rearrange("b s d -> s b d")
            sp.dma_start(grp(x_sb, 0), grp(xv, 0)).then_inc(s_x[0], 16)
            sp.dma_start(ctxT_sb[:, :, :], ctxT.rearrange("d (b c) -> d b c", b=B)).then_inc(s_ctx, 16)
            sp.dma_start(grp(x_sb, 1), grp(xv, 1)).then_inc(s_x[1], 16)
            sp.dma_start(gwT_sb[:, :], gwT).then_inc(s_gw, 16)
            half = E * H // 2
            for w_sb, w, s_w in ((w1_sb, w1T, s_w1), (w3_sb, w3T, s_w3), (w2_sb, w2T, s_w2)):
                for c in range(2):
                    sp.dma_start(w_sb[:, c * half:(c + 1) * half], w[:, c * half:(c + 1) * half]).then_inc(s_w, 16)
            rows = x2n_rows.rearrange("(b s) d -> s b d", s=S)
            base_rows = out[0:TOK, :].rearrange("(b s) d -> s b d", s=S)
            for g in range(G):
                sp.wait_ge(s_x2n, g + 1)
                sp.dma_start(grp(rows, g), grp(x2n, g)).then_inc(s_rows, 16)
                sp.dma_start(grp(base_rows, g), grp(x1, g)).then_inc(s_stored, 16)
            sp.dma_start(out[TOK:TOK + P, :], x1[:, 0, :]).then_inc(s_stored, 16)
            sp.wait_ge(s_rows, 32)

        @block.gpsimd
        def _(pool):
            nc.gpsimd.memset(ident[:, :], 0.0).then_inc(s_raw, 1)
            nc.gpsimd.memset(before[:, :], 1.0).then_inc(s_raw, 1)
            nc.gpsimd.memset(ones[:, :], 1.0).then_inc(s_const, 1)
            pool.wait_ge(s_raw, 2)
            nc.gpsimd.affine_select(out=ident[:, :], in_=ident[:, :], compare_op=ALU.not_equal, fill=1.0,
                                    base=0, pattern=[[-1, P]], channel_multiplier=1).then_inc(s_const, 1)
            nc.gpsimd.affine_select(out=before[:, :], in_=before[:, :], compare_op=ALU.is_gt, fill=0.0,
                                    base=0, pattern=[[1, P]], channel_multiplier=-1).then_inc(s_const, 1)
            for t, pattern, b, m in ((iota_lane, [[1, P]], 0, 0), (iota_tile, [[1, NT]], 0, 0),
                                     (iota_step, [[P, E]], 0, 0), (token_id, [[P, B]], 0, 1),
                                     (spare_row, [[0, 1]], TOK, 1)):
                nc.gpsimd.iota(t[:, :], pattern=pattern, base=b, channel_multiplier=m).then_inc(s_const, 1)

            def gather(p):
                pool.wait_ge(s_rows, 32)
                nc.gpsimd.indirect_dma_start(
                    xg[p][:, :], None, x2n_rows[:, :],
                    bass.IndirectOffsetOnAxis(ap=gid[p][:, 0:1], axis=0)).then_inc(s_gat[p], 16)

            pool.wait_ge(s_ids, 1)
            for p in range(2):
                nc.gpsimd.tensor_copy(gid[p][:, :], gather_id[:, p:p + 1]).then_inc(s_gid, 1)
            for p in range(2):
                pool.wait_ge(s_gid, p + 1)
                gather(p)

            def add_tile(i, p, free=True):
                pool.wait_ge(s_ids, 2)
                if free:
                    pool.wait_ge(s_add, 16 * i)
                nc.gpsimd.tensor_copy(aid[p][:, :], add_id[:, bass.ds(i, 1)]).then_inc(s_aid, 1)
                pool.wait_ge(s_ysb, i + 1)
                pool.wait_ge(s_aid, i + 1)
                pool.sem_inc(s_ready, 1)
                nc.gpsimd.indirect_dma_start(
                    out[:, :], bass.IndirectOffsetOnAxis(ap=aid[p][:, 0:1], axis=0), y_sb[p][:, :], None,
                    compute_op=ALU.add).then_inc(s_add, 16)

            def gather_next(i, p, gathers):
                pool.wait_ge(s_gat[p], gathers)
                nc.gpsimd.tensor_copy(gid[p][:, :], gather_id[:, bass.ds(i, 1)]).then_inc(s_gid, 1)
                pool.wait_ge(s_xT, i - 1)
                pool.wait_ge(s_gid, i + 1)
                pool.sem_inc(s_ready, 1)
                gather(p)

            n = pairs_of(pool)
            gather_next(2, 0, 16)
            gather_next(3, 1, 16)
            pool.wait_ge(s_stored, 48)
            add_tile(0, 0, False)
            with pool.Fori(1, n - 1) as j:
                gather_next(2 * j + 2, 0, 16 * j + 16)
                add_tile(2 * j - 1, 1)
                gather_next(2 * j + 3, 1, 16 * j + 16)
                add_tile(2 * j, 0)
            add_tile(2 * n - 3, 1)
            add_tile(2 * n - 2, 0)
            add_tile(2 * n - 1, 1)
            pool.wait_ge(s_add, 32 * n)

        @block.scalar
        def _(act):
            act.dma_start(wq_sb[:, :], wq).then_inc(s_wqkv, 16)
            act.dma_start(wk_sb[:, :], wk).then_inc(s_wqkv, 16)
            act.dma_start(wv_sb[:, :], wv).then_inc(s_wqkv, 16)
            act.dma_start(bq_sb[:, :], bq.rearrange("(d o) -> d o", o=1)).then_inc(s_wqkv, 16)
            act.dma_start(bk_sb[:, :], bk.rearrange("(d o) -> d o", o=1)).then_inc(s_wqkv, 16)
            act.dma_start(bv_sb[:, :], bv.rearrange("(o d) -> o d", o=1).broadcast_to([P, D])).then_inc(s_wqkv, 16)

            def rsqrt_start(n, g):
                k = n * G + g
                act.wait_ge(s_mv, k + 1)
                nc.scalar.activation(grp(lnvar[:, n], g), grp(meanvar[:, n], g)[:, :, 1], ACT.Ln,
                                     bias=eps_sb[:, 0:1]).then_inc(s_lnv, 1)
                act.wait_ge(s_lnv, k + 1)
                nc.scalar.activation(grp(rs0[:, n], g), grp(lnvar[:, n], g), ACT.Exp,
                                     scale=-0.5).then_inc(s_rs0, 1)

            def copy_kT(g):
                act.wait_ge(s_k, g + 1)
                nc.scalar.activation(grp(kT, g), ps_k[:, 0:TG * C], ACT.Identity,
                                     bias=bk_sb[:, 0:1]).then_inc(s_kT, 1)

            def copy_xnT(g):
                act.wait_ge(s_turn, g + 1)
                nc.scalar.activation(grp(xnT, g), ps_turn[:, :], ACT.Copy).then_inc(s_xnT, 1)

            def copy_qT(g):
                act.wait_ge(s_q, g + 1)
                nc.scalar.activation(grp(qT, g), ps_q[:, :], ACT.Identity,
                                     bias=bq_sb[:, 0:1]).then_inc(s_qT, 1)

            def softmax(g):
                act.wait_ge(s_nmax, g + 1)
                for t in range(g * TG, (g + 1) * TG):
                    k = t % TG
                    ins = nc.scalar.activation(probs[:, t, :], ps_s[:, k * C:(k + 1) * C], ACT.Exp,
                                               bias=nmax[:, t:t + 1], scale=SCALE,
                                               accum_out=psums[:, t:t + 1])
                ins.then_inc(s_probs, 1)

            def copy_pT(g):
                act.wait_ge(s_pTp, g + 1)
                nc.scalar.activation(grp(pT, g), ps_pT[0:C, :], ACT.Copy).then_inc(s_pT, 1)

            def copy_x2nT(g):
                act.wait_ge(s_turn2, g + 1)
                nc.scalar.activation(grp(x2nT, g), ps_turn[:, :], ACT.Copy).then_inc(s_x2nT, 1)

            act.wait_ge(s_zero, 3)
            rsqrt_start(0, 0)
            act.wait_ge(s_wqkv, 96)
            copy_kT(0)
            rsqrt_start(0, 1)
            copy_xnT(0)
            copy_kT(1)
            copy_qT(0)
            copy_xnT(1)
            softmax(0)
            copy_qT(1)
            copy_pT(0)
            softmax(1)
            rsqrt_start(1, 0)
            copy_pT(1)
            copy_x2nT(0)
            rsqrt_start(1, 1)
            copy_x2nT(1)
            act.wait_ge(s_vd, 1)
            nc.scalar.activation(vexp[:, :], vdiff[:, :], ACT.Exp).then_inc(s_ve, 1)

            def silu(i, q, free):
                act.wait_ge(s_a, i + 1)
                if free:
                    act.wait_ge(s_hid, i - 1)
                nc.scalar.activation(sil[q][:, :], ps_a[q][:, :], ACT.Silu).then_inc(s_sil, 1)

            def copy_hidT(i, p, free):
                act.wait_ge(s_hT, i + 1)
                if free:
                    act.wait_ge(s_y, i - 1)
                nc.scalar.activation(hidT[p][:, :], ps_hT[:, :], ACT.Copy).then_inc(s_hidT, 1)

            n = pairs_of(act)
            silu(0, 0, False)
            copy_hidT(0, 0, False)
            silu(1, 1, False)
            copy_hidT(1, 1, False)
            silu(2, 0, True)
            with act.Fori(1, n - 1) as j:
                for p in range(2):
                    copy_hidT(2 * j + p, p, True)
                    silu(2 * j + p + 1, 1 - p, True)
            copy_hidT(2 * n - 2, 0, True)
            silu(2 * n - 1, 1, True)
            copy_hidT(2 * n - 1, 1, True)

        @block.vector
        def _(dve):
            dve_ = nc.vector
            dve_.memset(eps_sb[:, :], EPS).then_inc(s_zero, 1)
            dve_.memset(member[:, B, :], 0.0).then_inc(s_zero, 1)
            dve_.memset(zeros8[:, :], 0.0).then_inc(s_zero, 1)

            def norm_stats(n, g, src):
                k = n * G + g
                for t in range(g * TG, (g + 1) * TG):
                    ins = dve_.bn_stats(stats[:, n, t, :], src[:, t, :])
                ins.then_inc(s_stat, 1)
                dve.wait_ge(s_stat, k + 1)
                for t in range(g * TG, (g + 1) * TG):
                    ins = dve_.bn_aggr(meanvar[:, n, t, :], stats[:, n, t, :])
                ins.then_inc(s_mv, 1)

            def normalise(n, g, src, dst, s_done):
                k = n * G + g
                y, v = grp(rs0[:, n], g), grp(meanvar[:, n], g)[:, :, 1]
                dve.wait_ge(s_rs0, k + 1)
                dve_.tensor_tensor(grp(nw1[:, n], g), y, y, ALU.mult).then_inc(s_newton, 1)
                dve.wait_ge(s_newton, 4 * k + 1)
                dve_.scalar_tensor_tensor(out=grp(nw2[:, n], g), in0=v, scalar=EPS, in1=grp(nw1[:, n], g),
                                          op0=ALU.add, op1=ALU.mult).then_inc(s_newton, 1)
                dve.wait_ge(s_newton, 4 * k + 2)
                dve_.tensor_scalar(grp(nw3[:, n], g), grp(nw2[:, n], g), -0.5, 1.5,
                                   ALU.mult, ALU.add).then_inc(s_newton, 1)
                dve.wait_ge(s_newton, 4 * k + 3)
                dve_.tensor_tensor(grp(rstd[:, n], g), y, grp(nw3[:, n], g), ALU.mult).then_inc(s_newton, 1)
                dve.wait_ge(s_newton, 4 * k + 4)
                for t in range(g * TG, (g + 1) * TG):
                    ins = dve_.tensor_scalar(dst[:, t, :], src[:, t, :], meanvar[:, n, t, 0:1],
                                             rstd[:, n, t:t + 1], ALU.subtract, ALU.mult)
                ins.then_inc(s_done, 1)

            def copy_v(g):
                dve.wait_ge(s_v, g + 1)
                dve_.tensor_tensor(grp(v_sb, g), ps_v[0:C, :].rearrange("p (t d) -> p t d", t=TG),
                                   bv_sb[0:C, :].unsqueeze(1).broadcast_to([C, TG, D]),
                                   ALU.add).then_inc(s_vsb, 1)

            def row_max(g):
                dve.wait_ge(s_score, g + 1)
                dve_.tensor_reduce(grp(smax, g), ps_s[:, 0:TG * C].rearrange("p (t c) -> p t c", t=TG),
                                   AX.X, ALU.max).then_inc(s_smax, 1)
                dve.wait_ge(s_smax, g + 1)
                dve_.tensor_scalar(grp(nmax, g), grp(smax, g), -SCALE, None, ALU.mult).then_inc(s_nmax, 1)

            def row_sum(g):
                dve.wait_ge(s_probs, g + 1)
                dve_.reciprocal(grp(rsum, g), grp(psums, g)).then_inc(s_rsum, 1)

            def residual(g):
                dve.wait_ge(s_rsum, g + 1)
                dve.wait_ge(s_av, g + 1)
                for t in range(g * TG, (g + 1) * TG):
                    k = t % TG
                    ins = dve_.scalar_tensor_tensor(out=x1[:, t, :], in0=ps_av[:, k * D:(k + 1) * D],
                                                    scalar=rsum[:, t:t + 1], in1=x_sb[:, t, :],
                                                    op0=ALU.mult, op1=ALU.add)
                ins.then_inc(s_x1, 1)
                dve.wait_ge(s_x1, g + 1)

            def top_two(g):
                dve.wait_ge(s_gate, g + 1)
                dve_.tensor_copy(grp(gate, g), ps_gate[g][:, 0:TG * E].rearrange("p (t e) -> p t e", t=TG))\
                    .then_inc(s_gsb, 1)
                dve.wait_ge(s_gsb, g + 1)
                for t in range(g * TG, (g + 1) * TG):
                    ins = dve_.max(top[:, t, :], gate[:, t, :])
                ins.then_inc(s_top, 1)
                dve.wait_ge(s_top, g + 1)
                for t in range(g * TG, (g + 1) * TG):
                    ins = dve_.max_index(topi[:, t, :], top[:, t, :], gate[:, t, :])
                ins.then_inc(s_topi, 1)

            for g in range(G):
                dve.wait_ge(s_x[g], 16)
                norm_stats(0, g, x_sb)
            normalise(0, 0, x_sb, xn, s_xn)
            normalise(0, 1, x_sb, xn, s_xn)
            dve.wait_ge(s_wqkv, 96)
            copy_v(0)
            copy_v(1)
            row_max(0)
            row_max(1)
            row_sum(0)
            residual(0)
            norm_stats(1, 0, x1)
            row_sum(1)
            normalise(1, 0, x1, x2n, s_x2n)
            residual(1)
            norm_stats(1, 1, x1)
            normalise(1, 1, x1, x2n, s_x2n)
            top_two(0)
            top_two(1)

            dve_.tensor_tensor(vdiff[:, :], top[:, :, 1], top[:, :, 0], ALU.subtract).then_inc(s_vd, 1)
            dve.wait_ge(s_topi, G)
            dve.wait_ge(s_const, 8)
            for c in range(K2):
                dve_.tensor_tensor(oh[:, c], iota_tile[:, 0:E].unsqueeze(1).broadcast_to([P, B, E]),
                                   topi[:, :, c].unsqueeze(2).broadcast_to([P, B, E]),
                                   ALU.is_equal).then_inc(s_oh, 1)
            dve.wait_ge(s_oh, 2)
            dve_.tensor_tensor(member[:, 0:B, :], oh[:, 0], oh[:, 1], ALU.add).then_inc(s_mem, 1)
            dve.wait_ge(s_ve, 1)
            dve_.tensor_scalar(vden[:, :], vexp[:, :], 1.0, None, ALU.add).then_inc(s_pw, 1)
            dve.wait_ge(s_pw, 1)
            dve_.reciprocal(pair_w[:, 0], vden[:, :]).then_inc(s_pw, 1)
            dve.wait_ge(s_pw, 2)
            dve_.tensor_tensor(pair_w[:, 1], vexp[:, :], pair_w[:, 0], ALU.mult).then_inc(s_pw, 1)

            route = [0]

            def link(ins):
                route[0] += 1
                ins.then_inc(s_route, 1)
                dve.wait_ge(s_route, route[0])

            dve.wait_ge(s_rank, 1)
            ranks = ps_rank[:, 0:(B + 1) * E].rearrange("p (b e) -> p b e", b=B + 1)
            link(dve_.tensor_tensor(over[:, :, :], ranks[:, B, :].unsqueeze(2).broadcast_to([P, E, E]),
                                    iota_step[:, :].unsqueeze(1).broadcast_to([P, E, E]), ALU.is_gt))
            link(dve_.tensor_reduce(ntile[:, :], over[:, :, :], AX.X, ALU.add))
            link(dve_.tensor_tensor_scan(tend[:, :], ntile[:, :], zeros8[:, :], 0.0, ALU.add, ALU.add))
            link(dve_.tensor_tensor(base[:, :], tend[:, :], ntile[:, :], ALU.subtract))
            link(dve_.scalar_tensor_tensor(out=rank[:, :, :], in0=base[:, :].unsqueeze(1).broadcast_to([P, B, E]),
                                           scalar=float(P), in1=ranks[:, 0:B, :], op0=ALU.mult, op1=ALU.add))
            for c in range(K2):
                ins = dve_.tensor_tensor(pick[:, c], oh[:, c], rank[:, :, :], ALU.mult)
            link(ins)
            link(dve_.tensor_reduce(slotf[:, :], pick[:, :, :, :].rearrange("p c b e -> p (c b) e"), AX.X, ALU.add))
            link(dve_.tensor_copy(slot[:, :], slotf[:, :]))
            link(dve_.tensor_scalar(stile[:, :], slot[:, :], 7, None, ALU.arith_shift_right))
            link(dve_.scalar_tensor_tensor(out=slane[:, :], in0=stile[:, :], scalar=float(-P), in1=slotf[:, :],
                                           op0=ALU.mult, op1=ALU.add))
            dve.wait_ge(s_pw, 3)
            dve_.tensor_tensor(tile_oh[:, :, 2, :], iota_tile[:, :].unsqueeze(1).broadcast_to([P, NPAIR, NT]),
                               stile[:, :].unsqueeze(2).broadcast_to([P, NPAIR, NT]),
                               ALU.is_equal).then_inc(s_tile, 1)
            dve.wait_ge(s_tile, 1)
            for c in range(K2):
                part = tile_oh[:, c * B:(c + 1) * B]
                dve_.tensor_tensor(part[:, :, 0, :], part[:, :, 2, :],
                                   token_id[:, :].unsqueeze(2).broadcast_to([P, B, NT]), ALU.mult)
                dve_.tensor_tensor(part[:, :, 1, :], part[:, :, 2, :],
                                   pair_w[:, c].unsqueeze(2).broadcast_to([P, B, NT]),
                                   ALU.mult).then_inc(s_tile, 1)
            for k in range(NPAIR):
                dve_.tensor_scalar(lane_oh[:, k, :], iota_lane[:, :], slane[:, k:k + 1], None,
                                   ALU.is_equal).then_inc(s_lane, 1)
            link(dve_.tensor_tensor(passed[:, :, :], tend[:, :].unsqueeze(1).broadcast_to([P, NT, E]),
                                    iota_tile[:, :].unsqueeze(2).broadcast_to([P, NT, E]), ALU.is_le))
            link(dve_.tensor_reduce(expf[:, :], passed[:, :, :], AX.X, ALU.add))
            link(dve_.tensor_scalar(tile_expert[:, :], expf[:, :], float(E - 1), None, ALU.min))
            link(dve_.tensor_scalar(tcount[:, :], tend[:, E - 1:E], -3.0, None, ALU.add))
            dve_.tensor_scalar(npairs_less2[:, :], tcount[:, :], 1, None, ALU.arith_shift_right).then_inc(s_tab, 1)
            dve.wait_ge(s_fill, 1)
            link(dve_.tensor_copy(filled[:, :, :], ps_fill[:, 0:3 * NT].rearrange("p (c t) -> p c t", c=3)))
            dve_.tensor_copy(gather_id[:, :], filled[:, 0, :]).then_inc(s_ids, 1)
            link(dve_.tensor_scalar(empty[:, :], filled[:, 2, :], -1.0, 1.0, ALU.mult, ALU.add))
            link(dve_.tensor_tensor(spare[:, :], empty[:, :], spare_row[:, 0:1].broadcast_to([P, NT]), ALU.mult))
            dve_.tensor_tensor(add_id[:, :], spare[:, :], filled[:, 0, :], ALU.add).then_inc(s_ids, 1)

            def copy_xT(i, p, free):
                dve.wait_ge(s_xT, i + 1)
                if free:
                    dve.wait_ge(s_b, i - 1)
                dve_.tensor_copy(xgT[p][:, :], ps_xT[:, 0:P]).then_inc(s_xgT, 1)

            def gate_mul(i, p, free):
                dve.wait_ge(s_sil, i + 1)
                dve.wait_ge(s_b, i + 1)
                if free:
                    dve.wait_ge(s_hT, i - 1)
                dve_.tensor_tensor(hid[p][:, :], ps_b[p][:, :], sil[p][:, :], ALU.mult).then_inc(s_hid, 1)

            def weigh(i, p, free):
                dve.wait_ge(s_y, i + 1)
                if free:
                    dve.wait_ge(s_add, 16 * i - 16)
                dve_.tensor_scalar(y_sb[p][:, :], ps_y[:, 0:D], filled[:, 1, bass.ds(i, 1)], None,
                                   ALU.mult).then_inc(s_ysb, 1)

            n = pairs_of(dve)
            copy_xT(0, 0, False)
            copy_xT(1, 1, False)
            gate_mul(0, 0, False)
            copy_xT(2, 0, True)
            gate_mul(1, 1, False)
            weigh(0, 0, False)
            copy_xT(3, 1, True)
            gate_mul(2, 0, True)
            weigh(1, 1, False)
            with dve.Fori(1, n - 1) as j:
                for p in range(2):
                    i = 2 * j + p
                    copy_xT(i + 2, p, True)
                    gate_mul(i + 1, 1 - p, True)
                    weigh(i, p, True)
            gate_mul(2 * n - 1, 1, True)
            weigh(2 * n - 2, 0, True)
            weigh(2 * n - 1, 1, True)

        @block.tensor
        def _(pe):
            mm = nc.tensor.matmul

            def keys(g):
                if g:
                    pe.wait_ge(s_kT, g)
                mm(ps_k[:, 0:TG * C], wk_sb[:, :], grp(ctxT_sb, g), start=True, stop=True).then_inc(s_k, 1)

            def values(g):
                if g:
                    pe.wait_ge(s_vsb, g)
                for t in range(g * TG, (g + 1) * TG):
                    k = t % TG
                    last = mm(ps_v[0:C, k * D:(k + 1) * D], ctxT_sb[:, t, :], wv_sb[:, :], start=True, stop=True)
                last.then_inc(s_v, 1)

            def turn(g, src, s_src, s_free, s_done):
                pe.wait_ge(s_src, g + 1)
                if s_free is not None:
                    pe.wait_ge(*s_free)
                for t in range(g * TG, (g + 1) * TG):
                    k = t % TG
                    last = nc.tensor.transpose(ps_turn[:, k * P:(k + 1) * P], src[:, t, :], ident[:, :])
                last.then_inc(s_done, 1)

            def queries(g):
                pe.wait_ge(s_xnT, g + 1)
                if g:
                    pe.wait_ge(s_qT, g)
                mm(ps_q[:, :], wq_sb[:, :], grp(xnT, g), start=True, stop=True).then_inc(s_q, 1)

            def scores(g):
                pe.wait_ge(s_qT, g + 1)
                pe.wait_ge(s_kT, g + 1)
                if g:
                    pe.wait_ge(s_probs, g)
                for t in range(g * TG, (g + 1) * TG):
                    k = t % TG
                    last = mm(ps_s[:, k * C:(k + 1) * C], qT[:, t, :], kT[:, t, :], start=True, stop=True)
                last.then_inc(s_score, 1)

            def turn_probs(g):
                pe.wait_ge(s_probs, g + 1)
                if g:
                    pe.wait_ge(s_pT, g)
                for t in range(g * TG, (g + 1) * TG):
                    k = t % TG
                    last = nc.tensor.transpose(ps_pT[0:C, k * P:(k + 1) * P], probs[:, t, :], ident[:, :])
                last.then_inc(s_pTp, 1)

            def attend(g):
                pe.wait_ge(s_pT, g + 1)
                pe.wait_ge(s_vsb, g + 1)
                if g:
                    pe.wait_ge(s_x1, g)
                for t in range(g * TG, (g + 1) * TG):
                    k = t % TG
                    last = mm(ps_av[:, k * D:(k + 1) * D], pT[:, t, :], v_sb[:, t, :], start=True, stop=True)
                last.then_inc(s_av, 1)

            def gates(g):
                pe.wait_ge(s_x2nT, g + 1)
                for t in range(g * TG, (g + 1) * TG):
                    k = t % TG
                    last = mm(ps_gate[g][:, k * E:(k + 1) * E], x2nT[:, t, :], gwT_sb[:, :], start=True, stop=True)
                last.then_inc(s_gate, 1)

            pe.wait_ge(s_const, 3)
            pe.wait_ge(s_ctx, 16)
            pe.wait_ge(s_wqkv, 96)
            keys(0)
            values(0)
            turn(0, xn, s_xn, None, s_turn)
            keys(1)
            queries(0)
            turn(1, xn, s_xn, (s_xnT, 1), s_turn)
            scores(0)
            queries(1)
            values(1)
            turn_probs(0)
            scores(1)
            attend(0)
            turn_probs(1)
            attend(1)
            turn(0, x2n, s_x2n, (s_xnT, 2), s_turn2)
            pe.wait_ge(s_gw, 16)
            gates(0)
            turn(1, x2n, s_x2n, (s_x2nT, 1), s_turn2)
            gates(1)

            pe.wait_ge(s_zero, 3)
            pe.wait_ge(s_mem, 1)
            ranks = ps_rank[:, 0:(B + 1) * E].rearrange("p (b e) -> p b e", b=B + 1)
            mm(ranks, before[:, :], member[:, :, :], start=True, stop=False)
            for t in range(B):
                last = mm(ranks[:, t + 1:, :], ones[:, :],
                          member[:, t, :].unsqueeze(1).broadcast_to([P, B - t, E]),
                          start=False, stop=(t == B - 1))
            last.then_inc(s_rank, 1)
            pe.wait_ge(s_vsb, 2)
            for k in range(NPAIR):
                pe.wait_ge(s_tile, 2 + k // B)
                pe.wait_ge(s_lane, k + 1)
                last = mm(ps_fill[:, 0:3 * NT], lane_oh[:, k, :], tile_oh[:, k].rearrange("p c t -> p (c t)"),
                          start=(k == 0), stop=(k == NPAIR - 1))
            last.then_inc(s_fill, 1)

            def turn_tokens(i, gathers, p, free=True):
                pe.wait_ge(s_gat[p], gathers)
                if free:
                    pe.wait_ge(s_xgT, i)
                nc.tensor.transpose(ps_xT[:, 0:P], xg[p][:, :], ident[:, :]).then_inc(s_xT, 1)

            def first(i, e, p, free):
                pe.wait_ge(s_xgT, i + 1)
                if free:
                    pe.wait_ge(s_sil, i - 1)
                mm(ps_a[p][:, :], xgT[p][:, :], w1_sb[:, bass.ds(e * H, H)], start=True, stop=True)\
                    .then_inc(s_a, 1)

            def second(i, e, p, free):
                if free:
                    pe.wait_ge(s_hid, i - 1)
                mm(ps_b[p][:, :], xgT[p][:, :], w3_sb[:, bass.ds(e * H, H)], start=True, stop=True)\
                    .then_inc(s_b, 1)

            def turn_hidden(i, p, free=True):
                pe.wait_ge(s_hid, i + 1)
                if free:
                    pe.wait_ge(s_hidT, i)
                for c in range(HC):
                    last = nc.tensor.transpose(ps_hT[:, c * P:(c + 1) * P], hid[p][:, c * P:(c + 1) * P], ident[:, :])
                last.then_inc(s_hT, 1)

            def third(i, e, p, free=True):
                pe.wait_ge(s_hidT, i + 1)
                if free:
                    pe.wait_ge(s_ysb, i)
                for c in range(HC):
                    last = mm(ps_y[:, 0:D], hidT[p][:, c * P:(c + 1) * P], w2_sb[:, bass.ds(e * H + c * D, D)],
                              start=(c == 0), stop=(c == HC - 1))
                last.then_inc(s_y, 1)

            def expert_of(i):
                return pe.value_load(tile_expert[0:1, bass.ds(i, 1)], min_val=0, max_val=E - 1)

            n = pairs_of(pe)
            turn_tokens(0, 16, 0, False)
            turn_tokens(1, 16, 1)
            pe.wait_ge(s_w1, 32)
            pe.wait_ge(s_w3, 32)
            pe.wait_ge(s_w2, 32)
            e0 = expert_of(0)
            first(0, e0, 0, False)
            second(0, e0, 0, False)
            def pair(j, free):
                e = [expert_of(2 * j + k) for k in range(3)]
                for p in range(2):
                    i = 2 * j + p
                    first(i + 1, e[p + 1], 1 - p, free or p)
                    turn_hidden(i, p, free or p)
                    turn_tokens(i + 2, 16 * j + 32, p)
                    second(i + 1, e[p + 1], 1 - p, free or p)
                    third(i, e[p], p, free or p)

            pair(0, False)
            with pe.Fori(1, n - 1) as j:
                pair(j, True)
            i = 2 * n - 2
            e = [expert_of(i + k) for k in range(2)]
            first(i + 1, e[1], 1, True)
            turn_hidden(i, 0)
            second(i + 1, e[1], 1, True)
            third(i, e[0], 0)
            turn_hidden(i + 1, 1)
            third(i + 1, e[1], 1)


def kernel(**inputs):
    import numpy as np
    import concourse.bacc as bacc
    from concourse.bass_utils import run_bass_kernel_spmd

    E, H, D = inputs["L0_ffn_w1"].shape
    P = 128
    arrays = {
        "x": inputs["x"],
        "ctxT": np.transpose(inputs["ctx_1024"], (2, 0, 1)).reshape(D, -1),
        "wq": inputs["L0_xattn_Wq"], "bq": inputs["L0_xattn_bq"],
        "wk": inputs["L0_xattn_Wk"], "bk": inputs["L0_xattn_bk"],
        "wv": inputs["L0_xattn_Wv"], "bv": inputs["L0_xattn_bv"],
        "gwT": np.transpose(inputs["L0_ffn_gate_w"]),
        "w1T": np.transpose(inputs["L0_ffn_w1"], (2, 0, 1)).reshape(D, E * H),
        "w3T": np.transpose(inputs["L0_ffn_w3"], (2, 0, 1)).reshape(D, E * H),
        "w2T": np.transpose(np.reshape(inputs["L0_ffn_w2"], (E, D, H // P, P)), (3, 0, 2, 1)).reshape(P, E * H),
    }
    nc = bacc.Bacc("TRN2", target_bir_lowering=False, num_devices=1)
    feeds, args = {}, []
    for name, a in arrays.items():
        a = np.ascontiguousarray(a)
        feeds[f"in_{name}"] = a
        args.append(nc.dram_tensor(f"in_{name}", a.shape, mybir.dt.from_np(a.dtype), kind="ExternalInput").ap())
    tokens = inputs["x"].shape[0] * inputs["x"].shape[1]
    res = nc.dram_tensor("out_rows", (tokens + P, D), F32, kind="ExternalOutput").ap()
    build(nc, *args, res)
    r = run_bass_kernel_spmd(nc, [feeds], core_ids=[0])
    return r.results[0]["out_rows"][:tokens].reshape(inputs["x"].shape)
```

```python
from contextlib import ExitStack

import concourse.bass as bass
from concourse import mybir

F32 = mybir.dt.float32
BF16 = mybir.dt.bfloat16
I32 = mybir.dt.int32
U32 = mybir.dt.uint32
ALU = mybir.AluOpType
ACT = mybir.ActivationFunctionType
AX = mybir.AxisListType

P = 128


def build(nc, x, ctxT, small, bv, w1T, w3T, w2T, out):
    B, S, D = x.shape
    C = ctxT.shape[1] // B
    E = small.shape[1] - 3 * D - 2
    H = w1T.shape[1] // E
    HC = H // P
    assert S == P and D == P and E == 8 and 4 * P <= 512 and H == 512
    G, TG = 2, B // 2
    TOK = B * S
    K2 = 2
    NPAIR = K2 * B
    NT = K2 * TOK // P + E + 2
    EPS = 1e-5
    SCALE = float(D) ** -0.5

    DR = D + K2
    tok_rows = nc.dram_tensor("tok_rows", [TOK, DR], F32, kind="Internal").ap()

    with ExitStack() as ctx:
        def sb(name, shape, dt=F32):
            return ctx.enter_context(nc.sbuf_tensor(name, shape, dt))

        def sem(name):
            return ctx.enter_context(nc.semaphore(name))

        bank = [ctx.enter_context(nc.psum_tensor(f"bank{i}", [P, 512], F32)) for i in range(8)]

        x_sb = sb("x_sb", [P, B, D])
        ctxT_sb = sb("ctxT_sb", [P, B, C])
        small_sb = sb("small_sb", [P, 3 * D + E + 2])
        wq_sb, wk_sb, wv_sb = (small_sb[:, c * D:(c + 1) * D] for c in range(3))
        gwT_sb = small_sb[:, 3 * D:3 * D + E]
        bq_sb = small_sb[:, 3 * D + E:3 * D + E + 1]
        bk_sb = small_sb[:, 3 * D + E + 1:3 * D + E + 2]
        bv_sb = sb("bv_sb", [P, D])
        w1_sb = sb("w1_sb", [P, E * H])
        w3_sb = sb("w3_sb", [P, E * H])
        w2_sb = sb("w2_sb", [P, E * H])
        ident = sb("ident", [P, P])
        before = sb("before", [P, P], BF16)
        ones = sb("ones", [P, P], BF16)
        iota_lane = sb("iota_lane", [P, P], BF16)
        iota_tile = sb("iota_tile", [P, NT], I32)
        iota_step = sb("iota_step", [P, E], I32)
        lane_id = sb("lane_id", [P, 1])
        tile_id = sb("tile_id", [P, B])
        iota_raw = sb("iota_raw", [P, P + 1 + B + NT], I32)
        iota_tilef = sb("iota_tilef", [P, NT])
        spare_row = sb("spare_row", [P, 1])
        minus_half = sb("minus_half", [P, B])
        zeros8 = sb("zeros8", [P, E])
        zero_w = sb("zero_w", [P, P], BF16)
        warm = sb("warm", [P, 1])
        stats = sb("stats", [P, 2, B, 6])
        meanvar = sb("meanvar", [P, 2, B, 2])
        vareps = sb("vareps", [P, 2, B])
        rstd = sb("rstd", [P, 2, B])
        xb = sb("xb", [P, B, D])
        xn = sb("xn", [P, B, D])
        xnT = sb("xnT", [P, B, P])
        qT = sb("qT", [P, B, P])
        kT = sb("kT", [P, B, C])
        v_sb = sb("v_sb", [C, B, D])
        smax = sb("smax", [P, B])
        nmax = sb("nmax", [P, B])
        probs = sb("probs", [P, B, C])
        psums = sb("psums", [P, B])
        rsum = sb("rsum", [P, B])
        pT = sb("pT", [C, B, P])
        x1 = sb("x1", [P, B, D])
        tok = sb("tok", [P, B, DR])
        x2n = tok[:, :, 0:D]
        x2nT = sb("x2nT", [P, B, P])
        gate = sb("gate", [P, B, E])
        top = sb("top", [P, B, 8])
        topi = sb("topi", [P, B, 8], U32)
        vdiff = sb("vdiff", [P, B])
        vexp = sb("vexp", [P, B])
        vden = sb("vden", [P, B])
        oh = sb("oh", [P, K2, B, E])
        member = sb("member", [P, B + 1, E], BF16)
        pick = sb("pick", [P, K2, B, E])
        rankf = sb("rankf", [P, K2, B])
        ranki = sb("ranki", [P, K2, B], I32)
        rtile = sb("rtile", [P, K2, B], I32)
        slane = sb("slane", [P, K2, B])
        lane_oh = sb("lane_oh", [P, K2, B, P], BF16)
        over = sb("over", [P, E, E])
        ntile = sb("ntile", [P, E])
        tend = sb("tend", [P, E])
        tbase = sb("tbase", [P, E])
        pickt = sb("pickt", [P, K2, B, E])
        ptile = sb("ptile", [P, K2, B])
        stile = sb("stile", [P, K2, B])
        tile_oh = sb("tile_oh", [P, K2, B, 3, NT], BF16)
        passed = sb("passed", [P, NT, E])
        expf = sb("expf", [P, NT])
        expc = sb("expc", [P, NT])
        pack2 = sb("pack2", [P, NT // 2])
        expert4 = sb("expert4", [P, NT // 2 - 1], I32)
        tcount = sb("tcount", [P, 1], I32)
        npairs_less3 = sb("npairs_less3", [P, 1], I32)
        slot_id = sb("slot_id", [P, NT])
        second_w = sb("second_w", [P, NT])
        first_w = sb("first_w", [P, NT])
        empty = sb("empty", [P, NT])
        spare = sb("spare", [P, NT])
        gather_id = sb("gather_id", [P, NT], U32)
        add_id = sb("add_id", [P, NT], U32)
        wpart = sb("wpart", [P, NT])
        slot_w = sb("slot_w", [P, NT])
        gid = [sb(f"gid{p}", [P, 1], U32) for p in range(2)]
        aid = [sb(f"aid{p}", [P, 1], U32) for p in range(2)]
        xg = [sb(f"xg{p}", [P, DR]) for p in range(2)]
        xgT = [sb(f"xgT{p}", [P, P]) for p in range(2)]
        sil = [sb(f"sil{p}", [P, H]) for p in range(2)]
        hid = [sb(f"hid{p}", [P, H]) for p in range(2)]
        hidT = [sb(f"hidT{p}", [P, H]) for p in range(2)]
        y_sb = [sb(f"y_sb{p}", [P, D]) for p in range(2)]

        ps_turn, ps_q, ps_k, ps_v, ps_s, ps_pT, ps_av, ps_rank = bank
        ps_gate = [ps_q, ps_k]
        ps_rank = [ps_pT, ps_rank]
        ps_fill = ps_v
        ps_xT, ps_y, ps_hT = bank[0], bank[3], bank[6]
        ps_a, ps_b = [bank[1], bank[2]], [bank[4], bank[5]]

        s_x = [sem(f"s_x_in{g}") for g in range(G)]
        s_small, s_bv = sem("s_small"), sem("s_bv")
        s_ctx = sem("s_ctx")
        s_w1, s_w3, s_w2 = sem("s_w1"), sem("s_w3"), sem("s_w2")
        s_raw = sem("s_raw")
        s_const = sem("s_const")
        s_zero, s_warm = sem("s_zero"), sem("s_warm")
        s_stat, s_mv, s_eps, s_rstd, s_xb = (sem(n) for n in ("s_stat", "s_mv", "s_eps", "s_rstd", "s_xb"))
        s_xn, s_x2n = sem("s_xn"), sem("s_x2n")
        s_turn, s_xnT = sem("s_turn"), sem("s_xnT")
        s_q, s_qT, s_k, s_kT, s_v, s_vsb = (sem(n) for n in ("s_q", "s_qT", "s_k", "s_kT", "s_v", "s_vsb"))
        s_score, s_smax, s_nmax, s_probs, s_rsum = (
            sem(n) for n in ("s_score", "s_smax", "s_nmax", "s_probs", "s_rsum"))
        s_pTp, s_pT, s_av, s_x1 = (sem(n) for n in ("s_pTp", "s_pT", "s_av", "s_x1"))
        s_turn2, s_x2nT, s_gate = sem("s_turn2"), sem("s_x2nT"), sem("s_gate")
        s_stored, s_rows = sem("s_stored"), sem("s_rows")
        s_vd, s_ve, s_pw = sem("s_vd"), sem("s_ve"), sem("s_pw")
        s_mem, s_rank, s_route = sem("s_mem"), sem("s_rank"), sem("s_route")
        s_lane, s_tile, s_fill, s_tab, s_ids, s_slot = (
            sem(n) for n in ("s_lane", "s_tile", "s_fill", "s_tab", "s_ids", "s_slot"))
        s_ready = sem("s_ready")
        s_gid, s_aid, s_gat = sem("s_gid"), sem("s_aid"), [sem(f"s_gat{p}") for p in range(2)]
        s_xT, s_xgT, s_a, s_b, s_sil, s_hid, s_hT, s_hidT, s_y, s_ysb, s_add = (
            sem(n) for n in ("s_xT", "s_xgT", "s_a", "s_b", "s_sil", "s_hid", "s_hT", "s_hidT",
                             "s_y", "s_ysb", "s_add"))
        s_wpart, s_wsel = sem("s_wpart"), sem("s_wsel")

        def grp(t, g):
            return t[:, g * TG:(g + 1) * TG]

        def pairs_of(eng):
            eng.wait_ge(s_tab, 1)
            return eng.value_load(npairs_less3[0:1, 0:1], min_val=TOK * K2 // P // 2 - 3,
                                  max_val=(NT - 2) // 2 - 3) + 3

        block = ctx.enter_context(nc.Block())

        @block.sync
        def _(sp):
            xv = x.rearrange("b s d -> s b d")
            cv = ctxT.rearrange("d (b c) -> d b c", b=B)
            sp.dma_start(grp(x_sb, 0), grp(xv, 0)).then_inc(s_x[0], 16)
            sp.dma_start(small_sb[:, :], small).then_inc(s_small, 16)
            sp.dma_start(ctxT_sb[:, :, :], cv).then_inc(s_ctx, 16)
            sp.dma_start(grp(x_sb, 1), grp(xv, 1)).then_inc(s_x[1], 16)
            sp.dma_start(bv_sb[:, :], bv.rearrange("(o d) -> o d", o=1).broadcast_to([P, D])).then_inc(s_bv, 16)
            half = E * H // 2
            for w_sb, w, s_w in ((w1_sb, w1T, s_w1), (w3_sb, w3T, s_w3), (w2_sb, w2T, s_w2)):
                for c in range(2):
                    sp.dma_start(w_sb[:, c * half:(c + 1) * half], w[:, c * half:(c + 1) * half]).then_inc(s_w, 16)
            rows = tok_rows.rearrange("(b s) d -> s b d", s=S)
            base_rows = out[0:TOK, :].rearrange("(b s) d -> s b d", s=S)
            for g in range(G):
                sp.wait_ge(s_x1, (g + 1) * TG)
                sp.dma_start(grp(base_rows, g), grp(x1, g)).then_inc(s_stored, 16)
            sp.dma_start(out[TOK:TOK + P, :], x1[:, 0, :]).then_inc(s_stored, 16)
            sp.wait_ge(s_x2n, B)
            sp.wait_ge(s_pw, 3)
            sp.dma_start(rows, tok[:, :, :]).then_inc(s_rows, 16)
            sp.wait_ge(s_stored, 48)
            sp.wait_ge(s_rows, 16)

        @block.gpsimd
        def _(pool):
            nc.gpsimd.memset(ident[:, :], 0.0).then_inc(s_raw, 1)
            nc.gpsimd.memset(before[:, :], 1.0).then_inc(s_raw, 1)
            nc.gpsimd.memset(ones[:, :], 1.0).then_inc(s_const, 1)
            nc.gpsimd.memset(minus_half[:, :], -0.5).then_inc(s_const, 1)
            nc.gpsimd.memset(zero_w[:, :], 0.0).then_inc(s_const, 1)
            pool.wait_ge(s_raw, 2)
            nc.gpsimd.affine_select(out=ident[:, :], in_=ident[:, :], compare_op=ALU.not_equal, fill=1.0,
                                    base=0, pattern=[[-1, P]], channel_multiplier=1).then_inc(s_const, 1)
            nc.gpsimd.affine_select(out=before[:, :], in_=before[:, :], compare_op=ALU.is_gt, fill=0.0,
                                    base=0, pattern=[[1, P]], channel_multiplier=-1).then_inc(s_const, 1)

            def rsqrt(n, g):
                k = n * G + g
                pool.wait_ge(s_const, 5)
                pool.wait_ge(s_eps, k + 1)
                nc.gpsimd.tensor_tensor(grp(rstd[:, n], g), grp(vareps[:, n], g), minus_half[:, 0:TG],
                                        ALU.pow).then_inc(s_rstd, 1)

            rsqrt(0, 0)
            for at, n, pattern, b, m in ((0, P, [[1, P]], 0, 0), (P, 1, [[0, 1]], 0, 1),
                                         (P + 1, B, [[P, B]], P, 0), (P + 1 + B, NT, [[1, NT]], 0, 0)):
                nc.gpsimd.iota(iota_raw[:, at:at + n], pattern=pattern, base=b,
                               channel_multiplier=m).then_inc(s_raw, 1)
            for t, pattern, b, m in ((iota_tile, [[1, NT]], 0, 0), (iota_step, [[P, E]], 0, 0)):
                nc.gpsimd.iota(t[:, :], pattern=pattern, base=b, channel_multiplier=m).then_inc(s_const, 1)
            rsqrt(0, 1)
            pool.wait_ge(s_raw, 6)
            for t, at in ((iota_lane, 0), (lane_id, P), (tile_id, P + 1), (iota_tilef, P + 1 + B)):
                nc.gpsimd.tensor_copy(t[:, :], iota_raw[:, at:at + t.shape[1]]).then_inc(s_const, 1)
            nc.gpsimd.tensor_scalar(spare_row[:, :], iota_raw[:, P:P + 1], float(TOK + P), None,
                                    ALU.add).then_inc(s_const, 1)
            pool.wait_ge(s_bv, 16)
            for g in range(G):
                pool.wait_ge(s_x[g], 16)
                nc.gpsimd.tensor_tensor(grp(xb, g), grp(x_sb, g), bv_sb[:, :].unsqueeze(1).broadcast_to([P, TG, D]),
                                        ALU.add).then_inc(s_xb, 1)
            rsqrt(1, 0)
            rsqrt(1, 1)

            def gather(p, ids):
                pool.wait_ge(s_rows, 16)
                nc.gpsimd.indirect_dma_start(
                    xg[p][:, :], None, tok_rows[:, :],
                    bass.IndirectOffsetOnAxis(ap=ids, axis=0)).then_inc(s_gat[p], 16)

            pool.wait_ge(s_ids, 1)
            for p in range(2):
                gather(p, gather_id[:, p:p + 1])

            def add_tile(i, p, free=True):
                pool.wait_ge(s_ids, 2)
                if free:
                    pool.wait_ge(s_add, 16 * i)
                nc.gpsimd.tensor_copy(aid[p][:, :], add_id[:, bass.ds(i, 1)]).then_inc(s_aid, 1)
                pool.wait_ge(s_ysb, i + 1)
                pool.wait_ge(s_aid, i + 1)
                pool.sem_inc(s_ready, 1)
                nc.gpsimd.indirect_dma_start(
                    out[:, :], bass.IndirectOffsetOnAxis(ap=aid[p][:, 0:1], axis=0), y_sb[p][:, :], None,
                    compute_op=ALU.add).then_inc(s_add, 16)

            def gather_next(i, p, gathers):
                pool.wait_ge(s_gat[p], gathers)
                nc.gpsimd.tensor_copy(gid[p][:, :], gather_id[:, bass.ds(i, 1)]).then_inc(s_gid, 1)
                pool.wait_ge(s_xT, i - 1)
                pool.wait_ge(s_wsel, i - 1)
                pool.wait_ge(s_gid, i - 1)
                pool.sem_inc(s_ready, 1)
                gather(p, gid[p][:, :])

            n = pairs_of(pool)
            gather_next(2, 0, 16)
            gather_next(3, 1, 16)
            pool.wait_ge(s_stored, 48)
            gather_next(4, 0, 32)
            add_tile(0, 0, False)
            with pool.Fori(1, n - 2) as j:
                gather_next(2 * j + 3, 1, 16 * j + 16)
                add_tile(2 * j - 1, 1)
                gather_next(2 * j + 4, 0, 16 * j + 32)
                add_tile(2 * j, 0)
            gather_next(2 * n - 1, 1, 16 * n - 16)
            add_tile(2 * n - 5, 1)
            add_tile(2 * n - 4, 0)
            add_tile(2 * n - 3, 1)
            add_tile(2 * n - 2, 0)
            add_tile(2 * n - 1, 1)
            pool.wait_ge(s_add, 32 * n)

        @block.scalar
        def _(act):
            def copy_kT(g):
                act.wait_ge(s_k, g + 1)
                nc.scalar.activation(grp(kT, g), ps_k[:, 0:TG * C], ACT.Identity,
                                     bias=bk_sb[:, 0:1]).then_inc(s_kT, 1)

            def copy_v(g):
                act.wait_ge(s_v, g + 1)
                nc.scalar.activation(grp(v_sb, g), ps_v[0:C, :], ACT.Copy).then_inc(s_vsb, 1)

            def copy_xnT(g):
                act.wait_ge(s_turn, g + 1)
                nc.scalar.activation(grp(xnT, g), ps_turn[:, :], ACT.Copy).then_inc(s_xnT, 1)

            def copy_qT(g):
                act.wait_ge(s_q, g + 1)
                nc.scalar.activation(grp(qT, g), ps_q[:, :], ACT.Identity,
                                     bias=bq_sb[:, 0:1]).then_inc(s_qT, 1)

            def softmax(g):
                act.wait_ge(s_nmax, g + 1)
                for t in range(g * TG, (g + 1) * TG):
                    k = t % TG
                    ins = nc.scalar.activation(probs[:, t, :], ps_s[:, k * C:(k + 1) * C], ACT.Exp,
                                               bias=nmax[:, t:t + 1], scale=SCALE,
                                               accum_out=psums[:, t:t + 1])
                    ins.then_inc(s_probs, 1)

            def copy_pT(g):
                act.wait_ge(s_pTp, g + 1)
                nc.scalar.activation(grp(pT, g), ps_pT[0:C, :], ACT.Copy).then_inc(s_pT, 1)

            def copy_x2nT(g):
                act.wait_ge(s_turn2, g + 1)
                nc.scalar.activation(grp(x2nT, g), ps_turn[:, :], ACT.Copy).then_inc(s_x2nT, 1)

            act.wait_ge(s_zero, 2)
            nc.scalar.activation(warm[:, :], zeros8[:, 0:1], ACT.Exp).then_inc(s_warm, 1)
            act.wait_ge(s_small, 16)
            copy_kT(0)
            copy_v(0)
            copy_xnT(0)
            copy_qT(0)
            copy_kT(1)
            copy_xnT(1)
            softmax(0)
            copy_pT(0)
            copy_qT(1)
            copy_v(1)
            softmax(1)
            copy_pT(1)
            copy_x2nT(0)
            copy_x2nT(1)
            act.wait_ge(s_vd, 1)
            nc.scalar.activation(vexp[:, :], vdiff[:, :], ACT.Exp).then_inc(s_ve, 1)
            act.wait_ge(s_warm, 1)
            nc.scalar.activation(warm[:, :], zeros8[:, 0:1], ACT.Silu).then_inc(s_warm, 1)

            def silu(i, q, free):
                act.wait_ge(s_a, i + 1)
                if free:
                    act.wait_ge(s_hid, i - 1)
                nc.scalar.activation(sil[q][:, :], ps_a[q][:, :], ACT.Silu).then_inc(s_sil, 1)

            def copy_hidT(i, p, free):
                act.wait_ge(s_hT, i + 1)
                if free:
                    act.wait_ge(s_y, i - 1)
                nc.scalar.activation(hidT[p][:, :], ps_hT[:, :], ACT.Copy).then_inc(s_hidT, 1)

            n = pairs_of(act)
            silu(0, 0, False)
            copy_hidT(0, 0, False)
            silu(1, 1, False)
            copy_hidT(1, 1, False)
            silu(2, 0, True)
            with act.Fori(1, n - 1) as j:
                for p in range(2):
                    copy_hidT(2 * j + p, p, True)
                    silu(2 * j + p + 1, 1 - p, True)
            copy_hidT(2 * n - 2, 0, True)
            silu(2 * n - 1, 1, True)
            copy_hidT(2 * n - 1, 1, True)

        @block.vector
        def _(dve):
            dve_ = nc.vector
            dve_.memset(member[:, B, :], 0.0).then_inc(s_zero, 1)
            dve_.memset(zeros8[:, :], 0.0).then_inc(s_zero, 1)

            def norm_stats(n, g, src):
                k = n * G + g
                for t in range(g * TG, (g + 1) * TG):
                    if n:
                        dve.wait_ge(s_x1, t + 1)
                    ins = dve_.bn_stats(stats[:, n, t, :], src[:, t, :])
                ins.then_inc(s_stat, 1)
                dve.wait_ge(s_stat, k + 1)
                for t in range(g * TG, (g + 1) * TG):
                    ins = dve_.bn_aggr(meanvar[:, n, t, :], stats[:, n, t, :])
                ins.then_inc(s_mv, 1)
                dve.wait_ge(s_mv, k + 1)
                dve_.tensor_scalar(grp(vareps[:, n], g), grp(meanvar[:, n], g)[:, :, 1], EPS, None,
                                   ALU.add).then_inc(s_eps, 1)

            def normalise(n, g, src, dst, s_done):
                dve.wait_ge(s_rstd, n * G + g + 1)
                for t in range(g * TG, (g + 1) * TG):
                    dve_.tensor_scalar(dst[:, t, :], src[:, t, :], meanvar[:, n, t, 0:1],
                                       rstd[:, n, t:t + 1], ALU.subtract, ALU.mult).then_inc(s_done, 1)

            def row_max(g):
                dve.wait_ge(s_score, g + 1)
                dve_.tensor_reduce(grp(smax, g), ps_s[:, 0:TG * C].rearrange("p (t c) -> p t c", t=TG),
                                   AX.X, ALU.max).then_inc(s_smax, 1)
                dve.wait_ge(s_smax, g + 1)
                dve_.tensor_scalar(grp(nmax, g), grp(smax, g), -SCALE, None, ALU.mult).then_inc(s_nmax, 1)

            def row_sum(g):
                dve.wait_ge(s_probs, (g + 1) * TG)
                dve_.reciprocal(grp(rsum, g), grp(psums, g)).then_inc(s_rsum, 1)

            def residual(g):
                dve.wait_ge(s_rsum, g + 1)
                dve.wait_ge(s_av, g + 1)
                dve.wait_ge(s_xb, g + 1)
                for t in range(g * TG, (g + 1) * TG):
                    k = t % TG
                    ins = dve_.scalar_tensor_tensor(out=x1[:, t, :], in0=ps_av[:, k * D:(k + 1) * D],
                                                    scalar=rsum[:, t:t + 1], in1=xb[:, t, :],
                                                    op0=ALU.mult, op1=ALU.add)
                    ins.then_inc(s_x1, 1)

            route = [0]

            def link(ins):
                route[0] += 1
                ins.then_inc(s_route, 1)
                dve.wait_ge(s_route, route[0])

            def of(t, g):
                return t[:, :, g * TG:(g + 1) * TG]

            def top_two(g):
                dve.wait_ge(s_gate, g + 1)
                link(dve_.tensor_copy(grp(gate, g), ps_gate[g][:, 0:TG * E].rearrange("p (t e) -> p t e", t=TG)))
                for t in range(g * TG, (g + 1) * TG):
                    ins = dve_.max(top[:, t, :], gate[:, t, :])
                link(ins)
                for t in range(g * TG, (g + 1) * TG):
                    ins = dve_.max_index(topi[:, t, :], top[:, t, :], gate[:, t, :])
                link(ins)
                link(dve_.tensor_tensor(
                    of(oh, g), iota_tile[:, 0:E].unsqueeze(1).unsqueeze(1).broadcast_to([P, K2, TG, E]),
                    grp(topi, g)[:, :, 0:K2].rearrange("p t c -> p c t").unsqueeze(3).broadcast_to([P, K2, TG, E]),
                    ALU.is_equal))
                dve_.tensor_tensor(grp(member, g), grp(oh[:, 0], g), grp(oh[:, 1], g), ALU.add).then_inc(s_mem, 1)

            def ranks_of(g):
                dve.wait_ge(s_rank, g + 1)
                r = ps_rank[g][:, 0:TG * E].rearrange("p (t e) -> p t e", t=TG)
                for c in range(K2):
                    ins = dve_.tensor_tensor(grp(pick[:, c], g), r, grp(oh[:, c], g), ALU.mult)
                link(ins)
                link(dve_.tensor_reduce(of(rankf, g), of(pick, g), AX.X, ALU.add))
                link(dve_.tensor_copy(of(ranki, g), of(rankf, g)))
                link(dve_.tensor_scalar(of(rtile, g), of(ranki, g), 7, None, ALU.arith_shift_right))
                link(dve_.scalar_tensor_tensor(out=of(slane, g), in0=of(rtile, g), scalar=float(-P),
                                               in1=of(rankf, g), op0=ALU.mult, op1=ALU.add))

            def lanes_of(g):
                for c in range(K2):
                    for t in range(g * TG, (g + 1) * TG):
                        dve_.tensor_scalar(lane_oh[:, c, t, :], iota_lane[:, :], slane[:, c, t:t + 1], None,
                                           ALU.is_equal).then_inc(s_lane, 1)

            dve.wait_ge(s_x[0], 16)
            norm_stats(0, 0, x_sb)
            dve.wait_ge(s_x[1], 16)
            normalise(0, 0, x_sb, xn, s_xn)
            norm_stats(0, 1, x_sb)
            normalise(0, 1, x_sb, xn, s_xn)
            row_max(0)
            row_max(1)
            row_sum(0)
            residual(0)
            norm_stats(1, 0, x1)
            row_sum(1)
            normalise(1, 0, x1, x2n, s_x2n)
            residual(1)
            norm_stats(1, 1, x1)
            normalise(1, 1, x1, x2n, s_x2n)
            dve.wait_ge(s_const, 12)
            top_two(0)
            ranks_of(0)
            lanes_of(0)
            top_two(1)

            dve_.tensor_tensor(vdiff[:, :], top[:, :, 1], top[:, :, 0], ALU.subtract).then_inc(s_vd, 1)
            dve.wait_ge(s_ve, 1)
            dve_.tensor_scalar(vden[:, :], vexp[:, :], 1.0, None, ALU.add).then_inc(s_pw, 1)
            dve.wait_ge(s_pw, 1)
            dve_.reciprocal(tok[:, :, D], vden[:, :]).then_inc(s_pw, 1)
            dve.wait_ge(s_pw, 2)
            dve_.tensor_tensor(tok[:, :, D + 1], vexp[:, :], tok[:, :, D], ALU.mult).then_inc(s_pw, 1)
            ranks_of(1)
            count = ps_rank[1][:, TG * E:(TG + 1) * E]
            link(dve_.tensor_tensor(over[:, :, :], count.unsqueeze(2).broadcast_to([P, E, E]),
                                    iota_step[:, :].unsqueeze(1).broadcast_to([P, E, E]), ALU.is_gt))
            link(dve_.tensor_reduce(ntile[:, :], over[:, :, :], AX.X, ALU.add))
            link(dve_.tensor_tensor_scan(tend[:, :], ntile[:, :], zeros8[:, :], 0.0, ALU.add, ALU.add))
            link(dve_.tensor_tensor(tbase[:, :], tend[:, :], ntile[:, :], ALU.subtract))
            link(dve_.tensor_tensor(pickt[:, :, :, :].rearrange("p c t e -> p (c t) e"),
                                    oh[:, :, :, :].rearrange("p c t e -> p (c t) e"),
                                    tbase[:, :].unsqueeze(1).broadcast_to([P, NPAIR, E]), ALU.mult))
            link(dve_.tensor_reduce(ptile[:, :, :], pickt[:, :, :, :], AX.X, ALU.add))
            link(dve_.tensor_tensor(stile[:, :, :], ptile[:, :, :], rtile[:, :, :], ALU.add))
            for c in range(K2):
                link(dve_.tensor_tensor(tile_oh[:, c, :, 2, :], iota_tilef[:, :].unsqueeze(1).broadcast_to([P, B, NT]),
                                        stile[:, c].unsqueeze(2).broadcast_to([P, B, NT]), ALU.is_equal))
                dve_.tensor_scalar(tile_oh[:, c, :, 0, :], tile_oh[:, c, :, 2, :], lane_id[:, 0:1], None, ALU.mult)
                dve_.tensor_tensor(tile_oh[:, c, :, 1, :], tile_oh[:, c, :, 2, :],
                                   tile_id[:, :].unsqueeze(2).broadcast_to([P, B, NT]),
                                   ALU.mult).then_inc(s_tile, 1)
            lanes_of(1)
            dve.wait_ge(s_fill, 1)
            dve_.tensor_scalar(gather_id[:, :], ps_fill[:, 0:NT], float(-P), 0.0, ALU.add, ALU.max).then_inc(s_ids, 1)
            link(dve_.tensor_scalar(tcount[:, :], tend[:, E - 1:E], -5.0, None, ALU.add))
            dve_.tensor_scalar(npairs_less3[:, :], tcount[:, :], 1, None, ALU.arith_shift_right).then_inc(s_tab, 1)
            link(dve_.tensor_tensor(passed[:, :, :], tend[:, :].unsqueeze(1).broadcast_to([P, NT, E]),
                                    iota_tile[:, :].unsqueeze(2).broadcast_to([P, NT, E]), ALU.is_le))
            link(dve_.tensor_reduce(expf[:, :], passed[:, :, :], AX.X, ALU.add))
            link(dve_.tensor_scalar(expc[:, :], expf[:, :], float(E - 1), None, ALU.min))
            link(dve_.scalar_tensor_tensor(out=pack2[:, :], in0=expc[:, 1:NT:2], scalar=float(E),
                                           in1=expc[:, 0:NT:2], op0=ALU.mult, op1=ALU.add))
            dve_.scalar_tensor_tensor(out=expert4[:, :], in0=pack2[:, 1:NT // 2], scalar=float(E * E),
                                      in1=pack2[:, 0:NT // 2 - 1], op0=ALU.mult, op1=ALU.add).then_inc(s_tab, 1)
            dve_.tensor_copy(second_w[:, :], ps_fill[:, NT:2 * NT]).then_inc(s_slot, 1)
            link(dve_.tensor_scalar(empty[:, :], ps_fill[:, 0:NT], 0.0, None, ALU.is_equal))
            dve.wait_ge(s_slot, 1)
            dve_.tensor_scalar(first_w[:, :], second_w[:, :], -1.0, 1.0, ALU.mult, ALU.add).then_inc(s_slot, 1)
            link(dve_.tensor_scalar(spare[:, :], empty[:, :], spare_row[:, 0:1], None, ALU.mult))
            link(dve_.scalar_tensor_tensor(out=slot_id[:, :], in0=ps_fill[:, 0:NT], scalar=float(-P),
                                           in1=spare[:, :], op0=ALU.add, op1=ALU.add))
            dve_.tensor_copy(add_id[:, :], slot_id[:, :]).then_inc(s_ids, 1)
            dve.wait_ge(s_slot, 2)

            def copy_xT(i, p, free):
                dve.wait_ge(s_xT, i + 1)
                if free:
                    dve.wait_ge(s_b, i - 1)
                dve_.tensor_copy(xgT[p][:, :], ps_xT[:, 0:P]).then_inc(s_xgT, 1)

            def pick_weight(i, p):
                dve.wait_ge(s_xT, i + 1)
                dve_.tensor_scalar(wpart[:, bass.ds(i, 1)], second_w[:, bass.ds(i, 1)], xg[p][:, D + 1:D + 2], None,
                                   ALU.mult).then_inc(s_wpart, 1)
                dve.wait_ge(s_wpart, i + 1)
                dve_.scalar_tensor_tensor(out=slot_w[:, bass.ds(i, 1)], in0=first_w[:, bass.ds(i, 1)],
                                          scalar=xg[p][:, D:D + 1], in1=wpart[:, bass.ds(i, 1)],
                                          op0=ALU.mult, op1=ALU.add).then_inc(s_wsel, 1)

            def gate_mul(i, p, free):
                dve.wait_ge(s_sil, i + 1)
                dve.wait_ge(s_b, i + 1)
                if free:
                    dve.wait_ge(s_hT, i - 1)
                dve_.tensor_tensor(hid[p][:, :], ps_b[p][:, :], sil[p][:, :], ALU.mult).then_inc(s_hid, 1)

            def weigh(i, p, free):
                dve.wait_ge(s_y, i + 1)
                if free:
                    dve.wait_ge(s_add, 16 * i - 16)
                dve.wait_ge(s_wsel, i + 1)
                dve_.tensor_scalar(y_sb[p][:, :], ps_y[:, 0:D], slot_w[:, bass.ds(i, 1)], None,
                                   ALU.mult).then_inc(s_ysb, 1)

            n = pairs_of(dve)
            copy_xT(0, 0, False)
            pick_weight(0, 0)
            copy_xT(1, 1, False)
            pick_weight(1, 1)
            gate_mul(0, 0, False)
            copy_xT(2, 0, True)
            pick_weight(2, 0)
            gate_mul(1, 1, False)
            weigh(0, 0, False)
            copy_xT(3, 1, True)
            pick_weight(3, 1)
            gate_mul(2, 0, True)
            weigh(1, 1, False)
            with dve.Fori(1, n - 1) as j:
                for p in range(2):
                    i = 2 * j + p
                    copy_xT(i + 2, p, True)
                    pick_weight(i + 2, p)
                    gate_mul(i + 1, 1 - p, True)
                    weigh(i, p, True)
            gate_mul(2 * n - 1, 1, True)
            weigh(2 * n - 2, 0, True)
            weigh(2 * n - 1, 1, True)

        @block.tensor
        def _(pe):
            mm = nc.tensor.matmul

            def keys(g):
                if g:
                    pe.wait_ge(s_kT, g)
                mm(ps_k[:, 0:TG * C], wk_sb, grp(ctxT_sb, g), start=True, stop=True).then_inc(s_k, 1)

            def values(g):
                if g:
                    pe.wait_ge(s_vsb, g)
                for t in range(g * TG, (g + 1) * TG):
                    k = t % TG
                    last = mm(ps_v[0:C, k * D:(k + 1) * D], ctxT_sb[:, t, :], wv_sb, start=True, stop=True)
                last.then_inc(s_v, 1)

            def turn(g, src, s_src, s_free, s_done):
                if s_free is not None:
                    pe.wait_ge(*s_free)
                for t in range(g * TG, (g + 1) * TG):
                    k = t % TG
                    pe.wait_ge(s_src, t + 1)
                    last = nc.tensor.transpose(ps_turn[:, k * P:(k + 1) * P], src[:, t, :], ident[:, :])
                last.then_inc(s_done, 1)

            def queries(g):
                pe.wait_ge(s_xnT, g + 1)
                if g:
                    pe.wait_ge(s_qT, g)
                mm(ps_q[:, :], wq_sb, grp(xnT, g), start=True, stop=True).then_inc(s_q, 1)

            def scores(g):
                pe.wait_ge(s_qT, g + 1)
                pe.wait_ge(s_kT, g + 1)
                if g:
                    pe.wait_ge(s_probs, g * TG)
                for t in range(g * TG, (g + 1) * TG):
                    k = t % TG
                    last = mm(ps_s[:, k * C:(k + 1) * C], qT[:, t, :], kT[:, t, :], start=True, stop=True)
                last.then_inc(s_score, 1)

            def turn_probs(g):
                if g:
                    pe.wait_ge(s_pT, g)
                for t in range(g * TG, (g + 1) * TG):
                    k = t % TG
                    pe.wait_ge(s_probs, t + 1)
                    last = nc.tensor.transpose(ps_pT[0:C, k * P:(k + 1) * P], probs[:, t, :], ident[:, :])
                last.then_inc(s_pTp, 1)

            def attend(g):
                pe.wait_ge(s_pT, g + 1)
                pe.wait_ge(s_vsb, g + 1)
                if g:
                    pe.wait_ge(s_x1, g * TG)
                for t in range(g * TG, (g + 1) * TG):
                    k = t % TG
                    last = mm(ps_av[:, k * D:(k + 1) * D], pT[:, t, :], v_sb[:, t, :], start=True, stop=True)
                last.then_inc(s_av, 1)

            def gates(g):
                pe.wait_ge(s_x2nT, g + 1)
                for t in range(g * TG, (g + 1) * TG):
                    k = t % TG
                    last = mm(ps_gate[g][:, k * E:(k + 1) * E], x2nT[:, t, :], gwT_sb, start=True, stop=True)
                last.then_inc(s_gate, 1)

            def count_before(g):
                pe.wait_ge(s_mem, g + 1)
                nb, lo = TG + g, g * TG
                tiles = TG * G if g else TG - 1
                r = ps_rank[g][:, 0:nb * E].rearrange("p (b e) -> p b e", b=nb)
                mm(r, before[:, :], member[:, lo:lo + nb, :], start=True, stop=False)
                for t in range(tiles):
                    later = max(t + 1 - lo, 0)
                    last = mm(r[:, later:, :], ones[:, :],
                              member[:, t, :].unsqueeze(1).broadcast_to([P, nb - later, E]),
                              start=False, stop=(t == tiles - 1))
                last.then_inc(s_rank, 1)

            pe.wait_ge(s_const, 5)
            pe.wait_ge(s_small, 16)
            pe.wait_ge(s_ctx, 16)
            keys(0)
            values(0)
            turn(0, xn, s_xn, None, s_turn)
            queries(0)
            keys(1)
            turn(1, xn, s_xn, (s_xnT, 1), s_turn)
            scores(0)
            queries(1)
            values(1)
            turn_probs(0)
            scores(1)
            attend(0)
            turn_probs(1)
            attend(1)
            turn(0, x2n, s_x2n, (s_xnT, 2), s_turn2)
            gates(0)
            pe.wait_ge(s_zero, 1)
            pe.wait_ge(s_pT, 2)
            count_before(0)
            turn(1, x2n, s_x2n, (s_x2nT, 1), s_turn2)
            gates(1)
            count_before(1)
            pe.wait_ge(s_vsb, 2)
            order = [(c, g * TG + k) for g in range(G) for c in range(K2) for k in range(TG)]
            for k, (c, t) in enumerate(order):
                pe.wait_ge(s_tile, c + 1)
                pe.wait_ge(s_lane, k + 1)
                if k == 0:
                    mm(ps_fill[:, 0:2 * NT], zero_w[:, :], tile_oh[:, c, t, 0:2].rearrange("p a t -> p (a t)"),
                       start=True, stop=False)
                mm(ps_fill[:, 0:NT], lane_oh[:, c, t, :], tile_oh[:, c, t, 0, :], start=False, stop=False)
                last = mm(ps_fill[:, 0:(1 + c) * NT], lane_oh[:, c, t, :],
                          tile_oh[:, c, t, 1:2 + c].rearrange("p a t -> p (a t)"),
                          start=False, stop=(k == NPAIR - 1))
            last.then_inc(s_fill, 1)

            def turn_tokens(i, gathers, p, free=True):
                pe.wait_ge(s_gat[p], gathers)
                if free:
                    pe.wait_ge(s_xgT, i)
                nc.tensor.transpose(ps_xT[:, 0:P], xg[p][:, 0:D], ident[:, :]).then_inc(s_xT, 1)

            def first(i, e, p, free):
                pe.wait_ge(s_xgT, i + 1)
                if free:
                    pe.wait_ge(s_sil, i - 1)
                mm(ps_a[p][:, :], xgT[p][:, :], w1_sb[:, bass.ds(e * H, H)], start=True, stop=True)\
                    .then_inc(s_a, 1)

            def second(i, e, p, free):
                if free:
                    pe.wait_ge(s_hid, i - 1)
                mm(ps_b[p][:, :], xgT[p][:, :], w3_sb[:, bass.ds(e * H, H)], start=True, stop=True)\
                    .then_inc(s_b, 1)

            def turn_hidden(i, p, free=True):
                pe.wait_ge(s_hid, i + 1)
                if free:
                    pe.wait_ge(s_hidT, i)
                for c in range(HC):
                    last = nc.tensor.transpose(ps_hT[:, c * P:(c + 1) * P], hid[p][:, c * P:(c + 1) * P], ident[:, :])
                last.then_inc(s_hT, 1)

            def third(i, e, p, free=True):
                pe.wait_ge(s_hidT, i + 1)
                if free:
                    pe.wait_ge(s_ysb, i)
                for c in range(HC):
                    last = mm(ps_y[:, 0:D], hidT[p][:, c * P:(c + 1) * P], w2_sb[:, bass.ds(e * H + c * D, D)],
                              start=(c == 0), stop=(c == HC - 1))
                last.then_inc(s_y, 1)

            def experts_of(j):
                w = pe.value_load(expert4[0:1, bass.ds(j, 1)], min_val=0, max_val=E ** 4 - 1)
                return [w % E, (w // E) % E, (w // E ** 2) % E, w // E ** 3]

            def pair(j, e, free=True, gathered=True):
                for p in range(2):
                    i = 2 * j + p
                    third(i, e[p], p, free or p)
                    first(i + 2, e[p + 2], p, True)
                    turn_hidden(i + 1, 1 - p)
                    if gathered or p == 0:
                        turn_tokens(i + 3, 16 * (j + 2 + p), 1 - p)
                    second(i + 2, e[p + 2], p, True)

            n = pairs_of(pe)
            turn_tokens(0, 16, 0, False)
            turn_tokens(1, 16, 1)
            pe.wait_ge(s_w1, 32)
            pe.wait_ge(s_w3, 32)
            pe.wait_ge(s_w2, 32)
            pe.wait_ge(s_tab, 2)
            e = experts_of(0)
            first(0, e[0], 0, False)
            second(0, e[0], 0, False)
            first(1, e[1], 1, False)
            turn_hidden(0, 0, False)
            turn_tokens(2, 32, 0)
            second(1, e[1], 1, False)
            pair(0, e, free=False)
            with pe.Fori(1, n - 2) as j:
                pair(j, experts_of(j))
            e = experts_of(n - 2)
            pair(n - 2, e, gathered=False)
            third(2 * n - 2, e[2], 0)
            turn_hidden(2 * n - 1, 1)
            third(2 * n - 1, e[3], 1)


def kernel(**inputs):
    import numpy as np
    import concourse.bacc as bacc
    from concourse.bass_utils import run_bass_kernel_spmd

    E, H, D = inputs["L0_ffn_w1"].shape
    P = 128
    arrays = {
        "x": inputs["x"],
        "ctxT": np.transpose(inputs["ctx_1024"], (2, 0, 1)).reshape(D, -1),
        "small": np.concatenate([inputs["L0_xattn_Wq"], inputs["L0_xattn_Wk"], inputs["L0_xattn_Wv"],
                                 np.transpose(inputs["L0_ffn_gate_w"]),
                                 inputs["L0_xattn_bq"][:, None], inputs["L0_xattn_bk"][:, None]], axis=1),
        "bv": inputs["L0_xattn_bv"],
        "w1T": np.transpose(inputs["L0_ffn_w1"], (2, 0, 1)).reshape(D, E * H),
        "w3T": np.transpose(inputs["L0_ffn_w3"], (2, 0, 1)).reshape(D, E * H),
        "w2T": np.transpose(np.reshape(inputs["L0_ffn_w2"], (E, D, H // P, P)), (3, 0, 2, 1)).reshape(P, E * H),
    }
    nc = bacc.Bacc("TRN2", target_bir_lowering=False, num_devices=1)
    feeds, args = {}, []
    for name, a in arrays.items():
        a = np.ascontiguousarray(a)
        feeds[f"in_{name}"] = a
        args.append(nc.dram_tensor(f"in_{name}", a.shape, mybir.dt.from_np(a.dtype), kind="ExternalInput").ap())
    tokens = inputs["x"].shape[0] * inputs["x"].shape[1]
    res = nc.dram_tensor("out_rows", (tokens + P, D), F32, kind="ExternalOutput").ap()
    build(nc, *args, res)
    r = run_bass_kernel_spmd(nc, [feeds], core_ids=[0])
    return r.results[0]["out_rows"][:tokens].reshape(inputs["x"].shape)
```

```python
from contextlib import ExitStack

import concourse.bass as bass
from concourse import mybir

F32 = mybir.dt.float32
BF16 = mybir.dt.bfloat16
F16 = mybir.dt.float16
F32R = mybir.dt.float32r
I32 = mybir.dt.int32
U32 = mybir.dt.uint32
ALU = mybir.AluOpType
ACT = mybir.ActivationFunctionType
AX = mybir.AxisListType

P = 128


def build(nc, x, ctxT, small, bv, w1T, w3T, w2T, out):
    B, S, D = x.shape
    C = ctxT.shape[1] // B
    E = small.shape[1] - 3 * D - 2
    H = w1T.shape[1] // E
    HC = H // P
    assert S == P and D == P and E == 8 and 4 * P <= 512 and H == 512
    G, TG = 2, B // 2
    TOK = B * S
    K2 = 2
    NPAIR = K2 * B
    NT = K2 * TOK // P + E + 2
    EPS = 1e-5
    SCALE = float(D) ** -0.5

    NW = -(-(NT - 2) // 8)

    DR = D + K2
    tok_rows = nc.dram_tensor("tok_rows", [TOK, DR], F32, kind="Internal").ap()

    with ExitStack() as ctx:
        def sb(name, shape, dt=F32):
            return ctx.enter_context(nc.sbuf_tensor(name, shape, dt))

        def sem(name):
            return ctx.enter_context(nc.semaphore(name))

        bank = [ctx.enter_context(nc.psum_tensor(f"bank{i}", [P, 512], F32)) for i in range(8)]

        x_sb = sb("x_sb", [P, B, D])
        ctxT_sb = sb("ctxT_sb", [P, B, C])
        small_sb = sb("small_sb", [P, 3 * D + E + 2])
        wq_sb, wk_sb, wv_sb = (small_sb[:, c * D:(c + 1) * D] for c in range(3))
        gwT_sb = small_sb[:, 3 * D:3 * D + E]
        bq_sb = small_sb[:, 3 * D + E:3 * D + E + 1]
        bk_sb = small_sb[:, 3 * D + E + 1:3 * D + E + 2]
        bv_sb = sb("bv_sb", [P, D])
        w1_sb = sb("w1_sb", [P, E * H])
        w3_sb = sb("w3_sb", [P, E * H])
        w2_sb = sb("w2_sb", [P, E * H])
        w_hi = [sb(f"w{k}_hi", [P, E * H], F32R) for k in (1, 3)]
        w_lo = [sb(f"w{k}_lo", [P, E * H], F32R) for k in (1, 3)]
        ident = sb("ident", [P, P])
        before = sb("before", [P, P], BF16)
        ones = sb("ones", [P, P], BF16)
        iota_lane = sb("iota_lane", [P, P], BF16)
        iota_tile = sb("iota_tile", [P, NT], I32)
        iota_step = sb("iota_step", [P, E], I32)
        token_id = sb("token_id", [P, B])
        iota_raw = sb("iota_raw", [P, P + B + NT + 1], I32)
        iota_tilef = sb("iota_tilef", [P, NT])
        spare_row = sb("spare_row", [P, 1])
        minus_half = sb("minus_half", [P, B])
        zeros8 = sb("zeros8", [P, E])
        warm = sb("warm", [P, 1])
        stats = sb("stats", [P, 2, B, 6])
        meanvar = sb("meanvar", [P, 2, B, 2])
        vareps = sb("vareps", [P, 2, B])
        rstd = sb("rstd", [P, 2, B])
        xb = sb("xb", [P, B, D])
        xn = sb("xn", [P, B, D])
        xnT = sb("xnT", [P, B, P])
        qT = sb("qT", [P, B, P])
        kT = sb("kT", [P, B, C])
        v_sb = sb("v_sb", [C, B, D])
        smax = sb("smax", [P, B])
        nmax = sb("nmax", [P, B])
        probs = sb("probs", [P, B, C])
        psums = sb("psums", [P, B])
        rsum = sb("rsum", [P, B])
        pT = sb("pT", [C, B, P])
        x1 = sb("x1", [P, B, D])
        tok = sb("tok", [P, B, DR])
        x2n = tok[:, :, 0:D]
        x2nT = sb("x2nT", [P, B, P])
        top = sb("top", [P, B, 8])
        topi = sb("topi", [P, B, 8], U32)
        vdiff = sb("vdiff", [P, B])
        vexp = sb("vexp", [P, B])
        vden = sb("vden", [P, B])
        oh = sb("oh", [P, K2, B, E])
        member = sb("member", [P, B + 1, E], BF16)
        pick = sb("pick", [P, K2, B, E])
        rank = sb("rank", [P, K2, B], I32)
        rtile = sb("rtile", [P, K2, B], I32)
        slane = sb("slane", [P, K2, B])
        lane_oh = sb("lane_oh", [P, K2, B, P], F16)
        over = sb("over", [P, E, E])
        ntile = sb("ntile", [P, E])
        tend = sb("tend", [P, E])
        tbase = sb("tbase", [P, E])
        pickt = sb("pickt", [P, K2, B, E])
        ptile = sb("ptile", [P, K2, B])
        stile = sb("stile", [P, K2, B])
        tile_oh = sb("tile_oh", [P, K2, B, 2, NT], F16)
        passed = sb("passed", [P, NT, E])
        expf = sb("expf", [P, NT])
        expc = sb("expc", [P, NT])
        pack2 = sb("pack2", [P, NT // 2])
        pack4 = sb("pack4", [P, NW, 2])
        expert_words = sb("expert_words", [P, NW], I32)
        tcount = sb("tcount", [P, 1], I32)
        same = sb("same", [P, NT])
        add_wait = sb("add_wait", [P, NT], I32)
        iota_adds = sb("iota_adds", [P, NT], I32)
        npairs_less3 = sb("npairs_less3", [P, 1], I32)
        slot_id = sb("slot_id", [P, NT])
        second_w = sb("second_w", [P, NT])
        first_w = sb("first_w", [P, NT])
        empty = sb("empty", [P, NT])
        spare = sb("spare", [P, NT])
        gather_id = sb("gather_id", [P, NT], U32)
        add_id = sb("add_id", [P, NT], U32)
        wpart = sb("wpart", [P, NT])
        slot_w = sb("slot_w", [P, NT])
        gid = [sb(f"gid{p}", [P, 1], U32) for p in range(2)]
        aid = [sb(f"aid{p}", [P, 1], U32) for p in range(2)]
        xg = [sb(f"xg{p}", [P, DR]) for p in range(2)]
        xgT = [sb(f"xgT{p}", [P, 2, P], F32R) for p in range(2)]
        sil = [sb(f"sil{p}", [P, H]) for p in range(2)]
        hid = [sb(f"hid{p}", [P, H]) for p in range(2)]
        hidT = [sb(f"hidT{p}", [P, H]) for p in range(2)]
        y_sb = [sb(f"y_sb{p}", [P, D]) for p in range(2)]

        ps_turn, ps_q, ps_k, ps_v, ps_s, ps_pT, ps_av, ps_rank = bank
        ps_xn, ps_q = [ps_turn, ps_av], [ps_q, ps_pT]
        ps_gate = [ps_q[0], ps_k]
        ps_s = [ps_s, ps_rank]
        ps_rank = [ps_pT, ps_rank]
        ps_x2n = [ps_turn, ps_v]
        ps_fill = ps_v
        ps_xT, ps_y = bank[0], bank[3]
        ps_hT = [bank[6], bank[7]]
        ps_a, ps_b = [bank[1], bank[2]], [bank[4], bank[5]]

        s_x = [sem(f"s_x_in{g}") for g in range(G)]
        s_small, s_bv = sem("s_small"), sem("s_bv")
        s_ctx = sem("s_ctx")
        s_w1, s_w3, s_w2 = sem("s_w1"), sem("s_w3"), sem("s_w2")
        s_raw = sem("s_raw")
        s_const = sem("s_const")
        s_ones, s_zero, s_warm = sem("s_ones"), sem("s_zero"), sem("s_warm")
        s_stat, s_mv, s_eps, s_rstd, s_xb = (sem(n) for n in ("s_stat", "s_mv", "s_eps", "s_rstd", "s_xb"))
        s_xn, s_x2n = sem("s_xn"), sem("s_x2n")
        s_turn, s_xnT = sem("s_turn"), sem("s_xnT")
        s_q, s_qT, s_k, s_kT, s_v, s_vsb = (sem(n) for n in ("s_q", "s_qT", "s_k", "s_kT", "s_v", "s_vsb"))
        s_score, s_smax, s_nmax, s_probs, s_rsum = (
            sem(n) for n in ("s_score", "s_smax", "s_nmax", "s_probs", "s_rsum"))
        s_pTp, s_pT, s_av, s_x1 = (sem(n) for n in ("s_pTp", "s_pT", "s_av", "s_x1"))
        s_turn2, s_x2nT, s_gate = sem("s_turn2"), sem("s_x2nT"), sem("s_gate")
        s_stored, s_rows = sem("s_stored"), sem("s_rows")
        s_vd, s_ve, s_pw = sem("s_vd"), sem("s_ve"), sem("s_pw")
        s_mem, s_rank, s_route = sem("s_mem"), sem("s_rank"), sem("s_route")
        s_slane, s_tile, s_fill, s_tab, s_ids, s_slot = (
            sem(n) for n in ("s_slane", "s_tile", "s_fill", "s_tab", "s_ids", "s_slot"))
        s_lane_pool, s_lane_dve = sem("s_lane_pool"), sem("s_lane_dve")
        s_ready = sem("s_ready")
        s_gid, s_aid, s_gat = sem("s_gid"), sem("s_aid"), [sem(f"s_gat{p}") for p in range(2)]
        s_xT, s_xgT, s_a, s_b, s_sil, s_hid, s_hT, s_hidT, s_y, s_ysb, s_clear = (
            sem(n) for n in ("s_xT", "s_xgT", "s_a", "s_b", "s_sil", "s_hid", "s_hT", "s_hidT",
                             "s_y", "s_ysb", "s_clear"))
        s_add = [sem("s_add0"), sem("s_add1")]
        s_same = sem("s_same")
        s_whi, s_wlo, s_xhi = (sem(n) for n in ("s_whi", "s_wlo", "s_xhi"))
        s_wpart, s_wsel = sem("s_wpart"), sem("s_wsel")

        def grp(t, g):
            return t[:, g * TG:(g + 1) * TG]

        def pairs_of(eng):
            eng.wait_ge(s_tab, 1)
            return eng.value_load(npairs_less3[0:1, 0:1], min_val=TOK * K2 // P // 2 - 3,
                                  max_val=(NT - 2) // 2 - 3) + 3

        CHOICES = (1, 0)

        fills = [[(c, g * TG + k) for c in CHOICES for k in range(TG)] for g in range(G)]
        NPOOL = 3

        def lane_one_hots(eng, pairs, s_done):
            for c, t in pairs:
                eng.tensor_scalar(lane_oh[:, c, t, :], iota_lane[:, :], slane[:, c, t:t + 1], None,
                                  ALU.is_equal).then_inc(s_done, 1)

        chunks = [(k, slice(e * H, (e + 1) * H)) for e in range(E) for k in range(2)]
        POOL_CHUNKS = 6
        w13 = (w1_sb, w3_sb)

        def low_part(eng, c):
            k, cols = chunks[c]
            return eng.tensor_tensor(w_lo[k][:, cols], w13[k][:, cols], w_hi[k][:, cols], ALU.subtract)

        block = ctx.enter_context(nc.Block())

        @block.sync
        def _(sp):
            xv = x.rearrange("b s d -> s b d")
            cv = ctxT.rearrange("d (b c) -> d b c", b=B)
            sp.dma_start(grp(x_sb, 0), grp(xv, 0)).then_inc(s_x[0], 16)
            sp.dma_start(grp(x_sb, 1), grp(xv, 1)).then_inc(s_x[1], 16)
            sp.dma_start(small_sb[:, :], small).then_inc(s_small, 16)
            sp.dma_start(ctxT_sb[:, :, :], cv).then_inc(s_ctx, 16)
            sp.dma_start(bv_sb[:, :], bv.rearrange("(o d) -> o d", o=1).broadcast_to([P, D])).then_inc(s_bv, 16)
            half = E * H // 2
            for w_sb, w, s_w in ((w1_sb, w1T, s_w1), (w3_sb, w3T, s_w3), (w2_sb, w2T, s_w2)):
                for c in range(2):
                    sp.dma_start(w_sb[:, c * half:(c + 1) * half], w[:, c * half:(c + 1) * half]).then_inc(s_w, 16)
            rows = tok_rows.rearrange("(b s) d -> s b d", s=S)
            base_rows = out[0:TOK, :].rearrange("(b s) d -> s b d", s=S)
            for g in range(G):
                sp.wait_ge(s_x1, (g + 1) * TG)
                sp.dma_start(grp(base_rows, g), grp(x1, g)).then_inc(s_stored, 16)
            sp.dma_start(out[TOK:TOK + P, :], x1[:, 0, :]).then_inc(s_stored, 16)
            sp.wait_ge(s_x2n, B)
            sp.wait_ge(s_pw, 3)
            sp.dma_start(rows, tok[:, :, :]).then_inc(s_rows, 16)
            sp.wait_ge(s_stored, 48)
            sp.wait_ge(s_rows, 16)

            def clear_adds(i, p):
                v = sp.value_load(add_wait[0:1, bass.ds(i, 1)], min_val=16, max_val=16 * (NT // 2))
                sp.wait_ge(s_add[1 - p], v)
                sp.sem_inc(s_clear, 1)

            n = pairs_of(sp)
            sp.wait_ge(s_tab, 3)
            sp.wait_ge(s_add[0], 16)
            sp.sem_inc(s_clear, 1)
            sp.wait_ge(s_add[1], 16)
            sp.sem_inc(s_clear, 1)
            clear_adds(3, 1)
            with sp.Fori(2, n) as j:
                clear_adds(2 * j, 0)
                clear_adds(2 * j + 1, 1)

        @block.gpsimd
        def _(pool):
            nc.gpsimd.memset(ident[:, :], 0.0).then_inc(s_raw, 1)
            nc.gpsimd.memset(before[:, :], 1.0).then_inc(s_raw, 1)
            nc.gpsimd.memset(minus_half[:, :], -0.5).then_inc(s_const, 1)
            pool.wait_ge(s_raw, 2)
            nc.gpsimd.affine_select(out=ident[:, :], in_=ident[:, :], compare_op=ALU.not_equal, fill=1.0,
                                    base=0, pattern=[[-1, P]], channel_multiplier=1).then_inc(s_const, 1)
            nc.gpsimd.affine_select(out=before[:, :], in_=before[:, :], compare_op=ALU.is_gt, fill=0.0,
                                    base=0, pattern=[[1, P]], channel_multiplier=-1).then_inc(s_const, 1)

            def rsqrt(n, g):
                k = n * G + g
                pool.wait_ge(s_const, 1)
                pool.wait_ge(s_eps, k + 1)
                nc.gpsimd.tensor_tensor(grp(rstd[:, n], g), grp(vareps[:, n], g), minus_half[:, 0:TG],
                                        ALU.pow).then_inc(s_rstd, 1)

            rsqrt(0, 0)
            rsqrt(0, 1)
            for at, n, pattern, b, m in ((0, P, [[1, P]], 0, 0), (P, B, [[P, B]], P, 1),
                                         (P + B, NT, [[1, NT]], 0, 0), (P + B + NT, 1, [[0, 1]], TOK + P, 1)):
                nc.gpsimd.iota(iota_raw[:, at:at + n], pattern=pattern, base=b,
                               channel_multiplier=m).then_inc(s_raw, 1)
            for t, pattern, b, m in ((iota_tile[:, :], [[1, NT]], 0, 0), (iota_step[:, :], [[P, E]], 0, 0),
                                     (iota_adds[:, 0:NT:2], [[16, NT // 2]], 0, 0),
                                     (iota_adds[:, 1:NT:2], [[16, NT // 2]], 16, 0)):
                nc.gpsimd.iota(t, pattern=pattern, base=b, channel_multiplier=m).then_inc(s_const, 1)
            pool.wait_ge(s_raw, 6)
            for t, at in ((iota_lane, 0), (token_id, P), (iota_tilef, P + B), (spare_row, P + B + NT)):
                nc.gpsimd.tensor_copy(t[:, :], iota_raw[:, at:at + t.shape[1]]).then_inc(s_const, 1)
            pool.wait_ge(s_bv, 16)
            for g in range(G):
                pool.wait_ge(s_x[g], 16)
                nc.gpsimd.tensor_tensor(grp(xb, g), grp(x_sb, g), bv_sb[:, :].unsqueeze(1).broadcast_to([P, TG, D]),
                                        ALU.add).then_inc(s_xb, 1)

            def low_parts(lo, hi):
                for c in range(lo, hi):
                    pool.wait_ge(s_whi, c + 1)
                    low_part(nc.gpsimd, c).then_inc(s_wlo, 1)

            rsqrt(1, 0)
            low_parts(0, 2)
            rsqrt(1, 1)
            low_parts(2, 4)

            pool.wait_ge(s_slane, 1)
            lane_one_hots(nc.gpsimd, fills[0], s_lane_pool)
            pool.wait_ge(s_slane, 2)
            lane_one_hots(nc.gpsimd, fills[1][:NPOOL], s_lane_pool)

            def gather(p, ids):
                pool.wait_ge(s_rows, 16)
                nc.gpsimd.indirect_dma_start(
                    xg[p][:, :], None, tok_rows[:, :],
                    bass.IndirectOffsetOnAxis(ap=ids, axis=0)).then_inc(s_gat[p], 16)

            pool.wait_ge(s_ids, 1)
            for p in range(2):
                gather(p, gather_id[:, p:p + 1])

            def add_ids(i, p, adds=None):
                if adds is not None:
                    pool.wait_ge(s_add[p], adds)
                nc.gpsimd.tensor_copy(aid[p][:, :], add_id[:, bass.ds(i, 1)]).then_inc(s_aid, 1)

            def add_tile(i, p, free=True):
                if free:
                    pool.wait_ge(s_clear, i)
                pool.wait_ge(s_ysb, i + 1)
                pool.wait_ge(s_aid, i + 1)
                pool.sem_inc(s_ready, 1)
                nc.gpsimd.indirect_dma_start(
                    out[:, :], bass.IndirectOffsetOnAxis(ap=aid[p][:, 0:1], axis=0), y_sb[p][:, :], None,
                    compute_op=ALU.add).then_inc(s_add[p], 16)

            def gather_ids(i, p, gathers=None):
                if gathers is not None:
                    pool.wait_ge(s_gat[p], gathers)
                nc.gpsimd.tensor_copy(gid[p][:, :], gather_id[:, bass.ds(i, 1)]).then_inc(s_gid, 1)

            def gather_next(i, p):
                pool.wait_ge(s_xT, i - 1)
                pool.wait_ge(s_wsel, i - 1)
                pool.wait_ge(s_gid, i - 1)
                pool.sem_inc(s_ready, 1)
                gather(p, gid[p][:, :])

            gather_ids(2, 0)
            gather_ids(3, 1)
            low_parts(4, POOL_CHUNKS)
            n = pairs_of(pool)
            gather_next(2, 0)
            gather_next(3, 1)
            gather_ids(4, 0, 32)
            pool.wait_ge(s_ids, 2)
            add_ids(0, 0)
            gather_next(4, 0)
            gather_ids(5, 1, 32)
            pool.wait_ge(s_stored, 48)
            add_tile(0, 0, False)
            add_ids(1, 1)
            gather_next(5, 1)
            gather_ids(6, 0, 48)
            add_tile(1, 1)
            add_ids(2, 0, 16)
            gather_next(6, 0)
            gather_ids(7, 1, 48)
            add_tile(2, 0)
            with pool.Fori(2, n - 2) as j:
                add_ids(2 * j - 1, 1, 16 * j - 16)
                gather_next(2 * j + 3, 1)
                gather_ids(2 * j + 4, 0, 16 * j + 32)
                add_tile(2 * j - 1, 1)
                add_ids(2 * j, 0, 16 * j)
                gather_next(2 * j + 4, 0)
                gather_ids(2 * j + 5, 1, 16 * j + 32)
                add_tile(2 * j, 0)
            add_ids(2 * n - 5, 1, 16 * n - 48)
            gather_next(2 * n - 1, 1)
            for k in range(5, 0, -1):
                add_tile(2 * n - k, k % 2)
                if k > 1:
                    add_ids(2 * n - k + 1, 1 - k % 2, 16 * (n - k // 2))
            pool.wait_ge(s_add[0], 16 * n)
            pool.wait_ge(s_add[1], 16 * n)

        @block.scalar
        def _(act):
            def copy_kT(g):
                act.wait_ge(s_k, g + 1)
                nc.scalar.activation(grp(kT, g), ps_k[:, 0:TG * C], ACT.Identity,
                                     bias=bk_sb[:, 0:1]).then_inc(s_kT, 1)

            def copy_v(g):
                act.wait_ge(s_v, g + 1)
                nc.scalar.activation(grp(v_sb, g), ps_v[0:C, :], ACT.Copy).then_inc(s_vsb, 1)

            def copy_xnT(g):
                act.wait_ge(s_turn, g + 1)
                nc.scalar.activation(grp(xnT, g), ps_xn[g][:, :], ACT.Copy).then_inc(s_xnT, 1)

            def copy_qT(g):
                act.wait_ge(s_q, g + 1)
                nc.scalar.activation(grp(qT, g), ps_q[g][:, :], ACT.Identity,
                                     bias=bq_sb[:, 0:1]).then_inc(s_qT, 1)

            def softmax(g):
                act.wait_ge(s_nmax, g + 1)
                for t in range(g * TG, (g + 1) * TG):
                    k = t % TG
                    ins = nc.scalar.activation(probs[:, t, :], ps_s[g][:, k * C:(k + 1) * C], ACT.Exp,
                                               bias=nmax[:, t:t + 1], scale=SCALE,
                                               accum_out=psums[:, t:t + 1])
                    ins.then_inc(s_probs, 1)

            def copy_pT(g):
                act.wait_ge(s_pTp, g + 1)
                nc.scalar.activation(grp(pT, g), ps_pT[0:C, :], ACT.Copy).then_inc(s_pT, 1)

            def copy_x2nT(g):
                for h in range(2):
                    act.wait_ge(s_turn2, 2 * g + h + 1)
                    t, w = g * TG + h * TG // 2, TG // 2
                    nc.scalar.activation(x2nT[:, t:t + w], ps_x2n[h][:, 0:w * P],
                                         ACT.Copy).then_inc(s_x2nT, 1)

            def high_parts(lo, hi):
                for c in range(lo, hi):
                    k, cols = chunks[c]
                    act.wait_ge((s_w1, s_w3)[k], 32)
                    nc.scalar.activation(w_hi[k][:, cols], w13[k][:, cols], ACT.Copy).then_inc(s_whi, 1)

            act.wait_ge(s_zero, 2)
            nc.scalar.activation(warm[:, :], zeros8[:, 0:1], ACT.Exp).then_inc(s_warm, 1)
            act.wait_ge(s_small, 16)
            copy_xnT(0)
            copy_kT(0)
            copy_xnT(1)
            copy_qT(0)
            copy_kT(1)
            softmax(0)
            copy_v(0)
            copy_pT(0)
            softmax(1)
            copy_pT(1)
            high_parts(0, 6)
            copy_x2nT(0)
            high_parts(6, 11)
            copy_x2nT(1)
            high_parts(11, 14)
            act.wait_ge(s_vd, 1)
            nc.scalar.activation(vexp[:, :], vdiff[:, :], ACT.Exp).then_inc(s_ve, 1)
            high_parts(14, 16)
            act.wait_ge(s_warm, 1)
            nc.scalar.activation(warm[:, :], zeros8[:, 0:1], ACT.Silu).then_inc(s_warm, 1)

            def silu(i, q, free):
                act.wait_ge(s_a, i + 1)
                if free:
                    act.wait_ge(s_hid, i - 1)
                nc.scalar.activation(sil[q][:, :], ps_a[q][:, :], ACT.Silu).then_inc(s_sil, 1)

            def copy_hidT(i, p, free):
                if free:
                    act.wait_ge(s_y, i - 1)
                for h in range(2):
                    act.wait_ge(s_hT, 2 * i + h + 1)
                    nc.scalar.activation(hidT[p][:, h * H // 2:(h + 1) * H // 2], ps_hT[h][:, 0:H // 2],
                                         ACT.Copy).then_inc(s_hidT, 1)

            n = pairs_of(act)
            silu(0, 0, False)
            copy_hidT(0, 0, False)
            silu(1, 1, False)
            copy_hidT(1, 1, False)
            silu(2, 0, True)
            with act.Fori(1, n - 1) as j:
                for p in range(2):
                    copy_hidT(2 * j + p, p, True)
                    silu(2 * j + p + 1, 1 - p, True)
            silu(2 * n - 1, 1, True)
            copy_hidT(2 * n - 2, 0, True)
            copy_hidT(2 * n - 1, 1, True)

        @block.vector
        def _(dve):
            dve_ = nc.vector
            dve_.memset(ones[:, :], 1.0).then_inc(s_ones, 1)
            dve_.memset(member[:, B, :], 0.0).then_inc(s_zero, 1)
            dve_.memset(zeros8[:, :], 0.0).then_inc(s_zero, 1)

            def norm_stats(n, g, src):
                k = n * G + g
                for t in range(g * TG, (g + 1) * TG):
                    if n:
                        dve.wait_ge(s_x1, t + 1)
                    ins = dve_.bn_stats(stats[:, n, t, :], src[:, t, :])
                ins.then_inc(s_stat, 1)
                dve.wait_ge(s_stat, k + 1)
                for t in range(g * TG, (g + 1) * TG):
                    ins = dve_.bn_aggr(meanvar[:, n, t, :], stats[:, n, t, :])
                ins.then_inc(s_mv, 1)
                dve.wait_ge(s_mv, k + 1)
                dve_.tensor_scalar(grp(vareps[:, n], g), grp(meanvar[:, n], g)[:, :, 1], EPS, None,
                                   ALU.add).then_inc(s_eps, 1)

            def normalise(n, g, src, dst, s_done):
                dve.wait_ge(s_rstd, n * G + g + 1)
                for t in range(g * TG, (g + 1) * TG):
                    dve_.tensor_scalar(dst[:, t, :], src[:, t, :], meanvar[:, n, t, 0:1],
                                       rstd[:, n, t:t + 1], ALU.subtract, ALU.mult).then_inc(s_done, 1)

            def row_max(g):
                dve.wait_ge(s_score, g + 1)
                dve_.tensor_reduce(grp(smax, g), ps_s[g][:, 0:TG * C].rearrange("p (t c) -> p t c", t=TG),
                                   AX.X, ALU.max).then_inc(s_smax, 1)
                dve.wait_ge(s_smax, g + 1)
                dve_.tensor_scalar(grp(nmax, g), grp(smax, g), -SCALE, None, ALU.mult).then_inc(s_nmax, 1)

            def row_sum(g):
                dve.wait_ge(s_probs, (g + 1) * TG)
                dve_.reciprocal(grp(rsum, g), grp(psums, g)).then_inc(s_rsum, 1)

            def residual(g):
                dve.wait_ge(s_rsum, g + 1)
                dve.wait_ge(s_av, g + 1)
                dve.wait_ge(s_xb, g + 1)
                for t in range(g * TG, (g + 1) * TG):
                    k = t % TG
                    ins = dve_.scalar_tensor_tensor(out=x1[:, t, :], in0=ps_av[:, k * D:(k + 1) * D],
                                                    scalar=rsum[:, t:t + 1], in1=xb[:, t, :],
                                                    op0=ALU.mult, op1=ALU.add)
                    ins.then_inc(s_x1, 1)

            route = [0]

            def link(ins, besides=0):
                route[0] += 1
                ins.then_inc(s_route, 1)
                dve.wait_ge(s_route, route[0] - besides)

            def of(t, g):
                return t[:, :, g * TG:(g + 1) * TG]

            def top_two(g):
                def gate(t):
                    return ps_gate[g][:, t % TG * E:(t % TG + 1) * E]

                dve.wait_ge(s_gate, g + 1)
                for t in range(g * TG, (g + 1) * TG):
                    ins = dve_.max(top[:, t, :], gate(t))
                link(ins)
                for t in range(g * TG, (g + 1) * TG):
                    ins = dve_.max_index(topi[:, t, :], top[:, t, :], gate(t))
                link(ins)
                link(dve_.tensor_tensor(
                    of(oh, g), iota_tile[:, 0:E].unsqueeze(1).unsqueeze(1).broadcast_to([P, K2, TG, E]),
                    grp(topi, g)[:, :, 0:K2].rearrange("p t c -> p c t").unsqueeze(3).broadcast_to([P, K2, TG, E]),
                    ALU.is_equal))
                dve_.tensor_tensor(grp(member, g), grp(oh[:, 0], g), grp(oh[:, 1], g), ALU.add).then_inc(s_mem, 1)

            def own_counts(g):
                r = ps_rank[g][:, 0:TG * E].rearrange("p (t e) -> p t e", t=TG)
                for c in range(K2):
                    ins = dve_.tensor_tensor(grp(pick[:, c], g), r, grp(oh[:, c], g), ALU.mult)
                return ins

            def rank_of(g):
                with nc.allow_low_precision("whole numbers below 2048"):
                    return dve_.tensor_reduce(of(rank, g), of(pick, g), AX.X, ALU.add)

            def rank_tile(g):
                return dve_.tensor_scalar(of(rtile, g), of(rank, g), 7, None, ALU.arith_shift_right)

            def rank_lane(g):
                return dve_.scalar_tensor_tensor(out=of(slane, g), in0=of(rtile, g), scalar=float(-P),
                                                 in1=of(rank, g), op0=ALU.mult, op1=ALU.add)

            def low_parts(lo, hi):
                for c in range(lo, hi):
                    dve.wait_ge(s_whi, c + 1)
                    low_part(dve_, c).then_inc(s_wlo, 1)

            dve.wait_ge(s_x[0], 16)
            norm_stats(0, 0, x_sb)
            dve.wait_ge(s_x[1], 16)
            norm_stats(0, 1, x_sb)
            normalise(0, 0, x_sb, xn, s_xn)
            normalise(0, 1, x_sb, xn, s_xn)
            row_max(0)
            dve.wait_ge(s_q, 2)
            dve_.tensor_scalar(grp(qT, 1), ps_q[1][:, :].rearrange("p (t s) -> p t s", t=TG), bq_sb[:, 0:1], None,
                               ALU.add).then_inc(s_qT, 1)
            row_max(1)
            row_sum(0)
            dve.wait_ge(s_v, 2)
            dve_.tensor_copy(grp(v_sb, 1), ps_v[0:C, :].rearrange("p (t d) -> p t d", t=TG)).then_inc(s_vsb, 1)
            residual(0)
            norm_stats(1, 0, x1)
            row_sum(1)
            residual(1)
            normalise(1, 0, x1, x2n, s_x2n)
            norm_stats(1, 1, x1)
            dve.wait_ge(s_const, 11)
            top_two(0)
            normalise(1, 1, x1, x2n, s_x2n)
            dve.wait_ge(s_rank, 1)
            link(own_counts(0))
            link(rank_of(0))
            link(rank_tile(0))
            rank_lane(0).then_inc(s_slane, 1)
            top_two(1)

            dve_.tensor_tensor(vdiff[:, :], top[:, :, 1], top[:, :, 0], ALU.subtract).then_inc(s_vd, 1)
            dve.wait_ge(s_ve, 1)
            dve_.tensor_scalar(vden[:, :], vexp[:, :], 1.0, None, ALU.add).then_inc(s_pw, 1)
            dve.wait_ge(s_pw, 1)
            dve_.reciprocal(tok[:, :, D], vden[:, :]).then_inc(s_pw, 1)
            dve.wait_ge(s_pw, 2)
            dve_.tensor_tensor(tok[:, :, D + 1], vexp[:, :], tok[:, :, D], ALU.mult).then_inc(s_pw, 1)
            dve.wait_ge(s_rank, 2)
            count = ps_rank[1][:, TG * E:(TG + 1) * E]
            link(own_counts(1))
            link(dve_.tensor_tensor(over[:, :, :], count.unsqueeze(2).broadcast_to([P, E, E]),
                                    iota_step[:, :].unsqueeze(1).broadcast_to([P, E, E]), ALU.is_gt), besides=1)
            link(rank_of(1), besides=1)
            link(dve_.tensor_reduce(ntile[:, :], over[:, :, :], AX.X, ALU.add), besides=1)
            link(rank_tile(1), besides=1)
            link(dve_.tensor_tensor_scan(tend[:, :], ntile[:, :], zeros8[:, :], 0.0, ALU.add, ALU.add), besides=1)
            rank_lane(1).then_inc(s_slane, 1)
            dve.wait_ge(s_route, route[0])
            link(dve_.tensor_tensor(tbase[:, :], tend[:, :], ntile[:, :], ALU.subtract))
            link(dve_.tensor_tensor(pickt[:, :, :, :].rearrange("p c t e -> p (c t) e"),
                                    oh[:, :, :, :].rearrange("p c t e -> p (c t) e"),
                                    tbase[:, :].unsqueeze(1).broadcast_to([P, NPAIR, E]), ALU.mult))
            link(dve_.tensor_reduce(ptile[:, :, :], pickt[:, :, :, :], AX.X, ALU.add))
            link(dve_.tensor_tensor(stile[:, :, :], ptile[:, :, :], rtile[:, :, :], ALU.add))
            for c in CHOICES:
                link(dve_.tensor_tensor(tile_oh[:, c, :, 1, :], iota_tilef[:, :].unsqueeze(1).broadcast_to([P, B, NT]),
                                        stile[:, c].unsqueeze(2).broadcast_to([P, B, NT]), ALU.is_equal))
                dve_.tensor_tensor(tile_oh[:, c, :, 0, :], tile_oh[:, c, :, 1, :],
                                   token_id[:, :].unsqueeze(2).broadcast_to([P, B, NT]),
                                   ALU.mult).then_inc(s_tile, 1)
            dve.wait_ge(s_slane, 2)
            lane_one_hots(dve_, fills[1][NPOOL:], s_lane_dve)
            link(dve_.tensor_scalar(tcount[:, :], tend[:, E - 1:E], -5.0, None, ALU.add))
            dve_.tensor_scalar(npairs_less3[:, :], tcount[:, :], 1, None, ALU.arith_shift_right).then_inc(s_tab, 1)
            dve.wait_ge(s_fill, 1)
            dve_.tensor_scalar(gather_id[:, :], ps_fill[:, 0:NT], float(-P), 0.0, ALU.add, ALU.max).then_inc(s_ids, 1)
            link(dve_.tensor_tensor(passed[:, :, :], tend[:, :].unsqueeze(1).broadcast_to([P, NT, E]),
                                    iota_tile[:, :].unsqueeze(2).broadcast_to([P, NT, E]), ALU.is_le))
            link(dve_.tensor_reduce(expf[:, :], passed[:, :, :], AX.X, ALU.add))
            dve_.tensor_tensor(same[:, 1:NT], expf[:, 1:NT], expf[:, 0:NT - 1], ALU.is_equal).then_inc(s_same, 1)
            link(dve_.tensor_scalar(expc[:, :], expf[:, :], float(E - 1), None, ALU.min))
            link(dve_.scalar_tensor_tensor(out=pack2[:, :], in0=expc[:, 1:NT:2], scalar=float(E),
                                           in1=expc[:, 0:NT:2], op0=ALU.mult, op1=ALU.add))
            link(dve_.scalar_tensor_tensor(out=pack4[:, :, :].rearrange("p w a -> p (w a)"),
                                           in0=pack2[:, 1:4 * NW:2], scalar=float(E ** 2),
                                           in1=pack2[:, 0:4 * NW:2], op0=ALU.mult, op1=ALU.add))
            dve_.scalar_tensor_tensor(out=expert_words[:, :], in0=pack4[:, :, 1], scalar=float(E ** 4),
                                      in1=pack4[:, :, 0], op0=ALU.mult, op1=ALU.add).then_inc(s_tab, 1)
            dve.wait_ge(s_same, 1)
            dve_.scalar_tensor_tensor(out=add_wait[:, 1:NT], in0=same[:, 1:NT], scalar=-16.0,
                                      in1=iota_adds[:, 1:NT], op0=ALU.mult, op1=ALU.add).then_inc(s_tab, 1)
            dve_.tensor_copy(second_w[:, :], ps_fill[:, NT:2 * NT]).then_inc(s_slot, 1)
            link(dve_.tensor_scalar(empty[:, :], ps_fill[:, 0:NT], 0.0, None, ALU.is_equal))
            dve.wait_ge(s_slot, 1)
            dve_.tensor_scalar(first_w[:, :], second_w[:, :], -1.0, 1.0, ALU.mult, ALU.add).then_inc(s_slot, 1)
            link(dve_.tensor_scalar(spare[:, :], empty[:, :], spare_row[:, 0:1], None, ALU.mult))
            link(dve_.scalar_tensor_tensor(out=slot_id[:, :], in0=ps_fill[:, 0:NT], scalar=float(-P),
                                           in1=spare[:, :], op0=ALU.add, op1=ALU.add))
            dve_.tensor_copy(add_id[:, :], slot_id[:, :]).then_inc(s_ids, 1)
            dve.wait_ge(s_slot, 2)

            def copy_xT(i, p, free):
                dve.wait_ge(s_xT, i + 1)
                if free:
                    dve.wait_ge(s_b, i - 1)
                dve_.tensor_copy(xgT[p][:, 0, :], ps_xT[:, 0:P]).then_inc(s_xhi, 1)
                dve.wait_ge(s_xhi, i + 1)
                dve_.tensor_tensor(xgT[p][:, 1, :], ps_xT[:, 0:P], xgT[p][:, 0, :], ALU.subtract).then_inc(s_xgT, 1)

            def pick_weight(i, p):
                dve.wait_ge(s_xT, i + 1)
                dve_.tensor_scalar(wpart[:, bass.ds(i, 1)], second_w[:, bass.ds(i, 1)], xg[p][:, D + 1:D + 2], None,
                                   ALU.mult).then_inc(s_wpart, 1)
                dve.wait_ge(s_wpart, i + 1)
                dve_.scalar_tensor_tensor(out=slot_w[:, bass.ds(i, 1)], in0=first_w[:, bass.ds(i, 1)],
                                          scalar=xg[p][:, D:D + 1], in1=wpart[:, bass.ds(i, 1)],
                                          op0=ALU.mult, op1=ALU.add).then_inc(s_wsel, 1)

            def gate_mul(i, p, free):
                dve.wait_ge(s_sil, i + 1)
                dve.wait_ge(s_b, i + 1)
                if free:
                    dve.wait_ge(s_hT, 2 * i - 2)
                dve_.tensor_tensor(hid[p][:, :], ps_b[p][:, :], sil[p][:, :], ALU.mult).then_inc(s_hid, 1)

            def weigh(i, p, adds=None):
                dve.wait_ge(s_y, i + 1)
                if adds is not None:
                    dve.wait_ge(s_add[p], adds)
                dve.wait_ge(s_wsel, i + 1)
                dve_.tensor_scalar(y_sb[p][:, :], ps_y[:, 0:D], slot_w[:, bass.ds(i, 1)], None,
                                   ALU.mult).then_inc(s_ysb, 1)

            n = pairs_of(dve)
            copy_xT(0, 0, False)
            pick_weight(0, 0)
            dve.wait_ge(s_wlo, POOL_CHUNKS)
            low_parts(POOL_CHUNKS, 7)
            copy_xT(1, 1, False)
            pick_weight(1, 1)
            low_parts(7, 8)
            gate_mul(0, 0, False)
            low_parts(8, 11)
            copy_xT(2, 0, True)
            pick_weight(2, 0)
            gate_mul(1, 1, False)
            weigh(0, 0)
            low_parts(11, 13)
            copy_xT(3, 1, True)
            pick_weight(3, 1)
            gate_mul(2, 0, True)
            weigh(1, 1)
            low_parts(13, 16)
            with dve.Fori(1, n - 1) as j:
                for p in range(2):
                    i = 2 * j + p
                    copy_xT(i + 2, p, True)
                    gate_mul(i + 1, 1 - p, True)
                    pick_weight(i + 2, p)
                    weigh(i, p, 16 * j)
            gate_mul(2 * n - 1, 1, True)
            weigh(2 * n - 2, 0, 16 * n - 16)
            weigh(2 * n - 1, 1, 16 * n - 16)

        @block.tensor
        def _(pe):
            mm = nc.tensor.matmul

            def keys(g):
                if g:
                    pe.wait_ge(s_kT, g)
                mm(ps_k[:, 0:TG * C], wk_sb, grp(ctxT_sb, g), start=True, stop=True).then_inc(s_k, 1)

            def values(g):
                if g:
                    pe.wait_ge(s_vsb, g)
                for t in range(g * TG, (g + 1) * TG):
                    k = t % TG
                    last = mm(ps_v[0:C, k * D:(k + 1) * D], ctxT_sb[:, t, :], wv_sb, start=True, stop=True)
                last.then_inc(s_v, 1)

            def turn_xn(g):
                for t in range(g * TG, (g + 1) * TG):
                    k = t % TG
                    pe.wait_ge(s_xn, t + 1)
                    last = nc.tensor.transpose(ps_xn[g][:, k * P:(k + 1) * P], xn[:, t, :], ident[:, :])
                last.then_inc(s_turn, 1)

            def turn_x2n(g):
                for h in range(2):
                    if g:
                        pe.wait_ge(s_x2nT, h + 1)
                    else:
                        pe.wait_ge(*((s_xnT, 2), (s_vsb, 2))[h])
                    for k in range(TG // 2):
                        t = g * TG + h * TG // 2 + k
                        pe.wait_ge(s_x2n, t + 1)
                        last = nc.tensor.transpose(ps_x2n[h][:, k * P:(k + 1) * P], x2n[:, t, :], ident[:, :])
                    last.then_inc(s_turn2, 1)

            def queries(g):
                pe.wait_ge(s_xnT, g + 1)
                mm(ps_q[g][:, :], wq_sb, grp(xnT, g), start=True, stop=True).then_inc(s_q, 1)

            def scores(g):
                pe.wait_ge(s_qT, g + 1)
                pe.wait_ge(s_kT, g + 1)
                for t in range(g * TG, (g + 1) * TG):
                    k = t % TG
                    last = mm(ps_s[g][:, k * C:(k + 1) * C], qT[:, t, :], kT[:, t, :], start=True, stop=True)
                last.then_inc(s_score, 1)

            def turn_probs(g):
                if g:
                    pe.wait_ge(s_pT, g)
                for t in range(g * TG, (g + 1) * TG):
                    k = t % TG
                    pe.wait_ge(s_probs, t + 1)
                    last = nc.tensor.transpose(ps_pT[0:C, k * P:(k + 1) * P], probs[:, t, :], ident[:, :])
                last.then_inc(s_pTp, 1)

            def attend(g):
                pe.wait_ge(s_pT, g + 1)
                pe.wait_ge(s_vsb, g + 1)
                if g:
                    pe.wait_ge(s_x1, g * TG)
                for t in range(g * TG, (g + 1) * TG):
                    k = t % TG
                    last = mm(ps_av[:, k * D:(k + 1) * D], pT[:, t, :], v_sb[:, t, :], start=True, stop=True)
                last.then_inc(s_av, 1)

            def gates(g):
                for t in range(g * TG, (g + 1) * TG):
                    k = t % TG
                    pe.wait_ge(s_x2nT, 2 * g + k * 2 // TG + 1)
                    last = mm(ps_gate[g][:, k * E:(k + 1) * E], x2nT[:, t, :], gwT_sb, start=True, stop=True)
                last.then_inc(s_gate, 1)

            def count_before(g):
                pe.wait_ge(s_mem, g + 1)
                nb, lo = TG + g, g * TG
                tiles = TG * G if g else TG - 1
                r = ps_rank[g][:, 0:nb * E].rearrange("p (b e) -> p b e", b=nb)
                mm(r, before[:, :], member[:, lo:lo + nb, :], start=True, stop=False)
                for t in range(tiles):
                    later = max(t + 1 - lo, 0)
                    last = mm(r[:, later:, :], ones[:, :],
                              member[:, t, :].unsqueeze(1).broadcast_to([P, nb - later, E]),
                              start=False, stop=(t == tiles - 1))
                last.then_inc(s_rank, 1)

            def keep_busy(bank, n):
                for _ in range(n):
                    mm(bank[:, :], ones[:, :], ones[:, :].unsqueeze(1).broadcast_to([P, 4, P]),
                       start=True, stop=True)

            pe.wait_ge(s_ones, 1)
            keep_busy(ps_rank[1], 14)
            pe.wait_ge(s_const, 3)
            pe.wait_ge(s_small, 16)
            pe.wait_ge(s_ctx, 16)
            turn_xn(0)
            keys(0)
            turn_xn(1)
            queries(0)
            keys(1)
            scores(0)
            queries(1)
            values(0)
            scores(1)
            turn_probs(0)
            values(1)
            attend(0)
            keep_busy(ps_k, 2)
            turn_probs(1)
            attend(1)
            keep_busy(ps_k, 6)
            turn_x2n(0)
            gates(0)
            keep_busy(ps_k, 8)
            turn_x2n(1)
            pe.wait_ge(s_zero, 1)
            pe.wait_ge(s_pT, 2)
            count_before(0)
            gates(1)
            keep_busy(ps_rank[1], 4)
            count_before(1)
            keep_busy(ps_av, 14)
            pe.wait_ge(s_vsb, 2)
            order = fills[0] + fills[1]
            for k, (c, t) in enumerate(order):
                pe.wait_ge(s_tile, CHOICES.index(c) + 1)
                if k < len(fills[0]) + NPOOL:
                    pe.wait_ge(s_lane_pool, k + 1)
                else:
                    pe.wait_ge(s_lane_dve, k + 1 - len(fills[0]) - NPOOL)
                mine = (1 + c) * NT
                last = mm(ps_fill[:, 0:mine], lane_oh[:, c, t, :],
                          tile_oh[:, c, t, 0:1 + c].rearrange("p a t -> p (a t)"),
                          start=(k == 0), stop=(k == NPAIR - 1))
                if k % TG == TG - 1 and k < NPAIR - TG:
                    keep_busy(ps_av, 1)
            last.then_inc(s_fill, 1)

            keep_busy(ps_av, 15)

            def turn_tokens(i, gathers, p, free=True):
                pe.wait_ge(s_gat[p], gathers)
                if free:
                    pe.wait_ge(s_xgT, i)
                nc.tensor.transpose(ps_xT[:, 0:P], xg[p][:, 0:D], ident[:, :]).then_inc(s_xT, 1)

            def split_product(ps, xT, k, e):
                cols = bass.ds(e * H, H)
                mm(ps[:, :], xT[:, 1, :], w_hi[k][:, cols], start=True, stop=False)
                mm(ps[:, :], xT[:, 0, :], w_lo[k][:, cols], start=False, stop=False)
                return mm(ps[:, :], xT[:, 0, :], w_hi[k][:, cols], start=False, stop=True)

            def first(i, e, p, free, split=True):
                if not split:
                    pe.wait_ge(s_wlo, 2 * e + 2)
                pe.wait_ge(s_xgT, i + 1)
                if free:
                    pe.wait_ge(s_sil, i - 1)
                split_product(ps_a[p], xgT[p], 0, e).then_inc(s_a, 1)

            def second(i, e, p, free):
                if free:
                    pe.wait_ge(s_hid, i - 1)
                split_product(ps_b[p], xgT[p], 1, e).then_inc(s_b, 1)

            def turn_hidden(i, p, free=True):
                pe.wait_ge(s_hid, i + 1)
                if free:
                    pe.wait_ge(s_hidT, 2 * i)
                for c in range(HC):
                    k = c % (HC // 2)
                    ins = nc.tensor.transpose(ps_hT[c // (HC // 2)][:, k * P:(k + 1) * P],
                                              hid[p][:, c * P:(c + 1) * P], ident[:, :])
                    if k == HC // 2 - 1:
                        ins.then_inc(s_hT, 1)

            def third(i, e, p, free=True):
                pe.wait_ge(s_hidT, 2 * i + 2)
                if free:
                    pe.wait_ge(s_ysb, i)
                for c in range(HC):
                    last = mm(ps_y[:, 0:D], hidT[p][:, c * P:(c + 1) * P], w2_sb[:, bass.ds(e * H + c * D, D)],
                              start=(c == 0), stop=(c == HC - 1))
                last.then_inc(s_y, 1)

            word = [pe.alloc_register(f"expert_word{k}") for k in range(NW)]

            def load_word(k):
                pe.reg_mov(word[k], pe.value_load(expert_words[0:1, k:k + 1], min_val=0, max_val=E ** 8 - 1))

            def experts_in(w):
                return [(w // E ** k) % E for k in range(4)]

            def next_experts():
                w = [pe.snap(r, min_val=0, max_val=E ** 8 - 1) for r in word]
                return w, experts_in(w[0])

            def shift_word(w, k):
                more = (w[k + 1] % E ** 2) * E ** 6 if k < NW - 1 else 0
                pe.reg_mov(word[k], w[k] // E ** 2 + more)

            def pair(j, free=True, split=True, gathered=True):
                w, e = next_experts()
                for p in range(2):
                    i = 2 * j + p
                    third(i, e[p], p, free or p)
                    first(i + 2, e[p + 2], p, True, split)
                    shift_word(w, p)
                    turn_hidden(i + 1, 1 - p)
                    if gathered or p == 0:
                        turn_tokens(i + 3, 16 * (j + 2 + p), 1 - p)
                    second(i + 2, e[p + 2], p, True)
                    if p == 0:
                        shift_word(w, 2)
                return e

            n = pairs_of(pe)
            pe.wait_ge(s_w2, 32)
            pe.wait_ge(s_tab, 2)
            load_word(0)
            e = experts_in(pe.snap(word[0], min_val=0, max_val=E ** 8 - 1))
            turn_tokens(0, 16, 0, False)
            load_word(1)
            first(0, e[0], 0, False, False)
            turn_tokens(1, 16, 1)
            second(0, e[0], 0, False)
            first(1, e[1], 1, False, False)
            load_word(2)
            turn_hidden(0, 0, False)
            turn_tokens(2, 32, 0)
            second(1, e[1], 1, False)
            pair(0, free=False, split=False)
            pair(1, split=False)
            pe.wait_ge(s_wlo, 2 * E)
            with pe.Fori(2, n - 2) as j:
                pair(j)
            e = pair(n - 2, gathered=False)
            third(2 * n - 2, e[2], 0)
            turn_hidden(2 * n - 1, 1)
            third(2 * n - 1, e[3], 1)


def kernel(**inputs):
    import numpy as np
    import concourse.bacc as bacc
    from concourse.bass_utils import run_bass_kernel_spmd

    E, H, D = inputs["L0_ffn_w1"].shape
    P = 128
    arrays = {
        "x": inputs["x"],
        "ctxT": np.transpose(inputs["ctx_1024"], (2, 0, 1)).reshape(D, -1),
        "small": np.concatenate([inputs["L0_xattn_Wq"], inputs["L0_xattn_Wk"], inputs["L0_xattn_Wv"],
                                 np.transpose(inputs["L0_ffn_gate_w"]),
                                 inputs["L0_xattn_bq"][:, None], inputs["L0_xattn_bk"][:, None]], axis=1),
        "bv": inputs["L0_xattn_bv"],
        "w1T": np.transpose(inputs["L0_ffn_w1"], (2, 0, 1)).reshape(D, E * H),
        "w3T": np.transpose(inputs["L0_ffn_w3"], (2, 0, 1)).reshape(D, E * H),
        "w2T": np.transpose(np.reshape(inputs["L0_ffn_w2"], (E, D, H // P, P)), (3, 0, 2, 1)).reshape(P, E * H),
    }
    nc = bacc.Bacc("TRN2", target_bir_lowering=False, num_devices=1)
    feeds, args = {}, []
    for name, a in arrays.items():
        a = np.ascontiguousarray(a)
        feeds[f"in_{name}"] = a
        args.append(nc.dram_tensor(f"in_{name}", a.shape, mybir.dt.from_np(a.dtype), kind="ExternalInput").ap())
    tokens = inputs["x"].shape[0] * inputs["x"].shape[1]
    res = nc.dram_tensor("out_rows", (tokens + P, D), F32, kind="ExternalOutput").ap()
    build(nc, *args, res)
    r = run_bass_kernel_spmd(nc, [feeds], core_ids=[0])
    return r.results[0]["out_rows"][:tokens].reshape(inputs["x"].shape)
```
